# Optimizing a Trainium2 kernel written in Bass

```python
import numpy as np
import jax
import jax.numpy as jnp

def _softmax(x, axis=-1):
    return jax.nn.softmax(x, axis=axis)

def _gelu(x):
    return jax.nn.gelu(x, approximate=True)

def _silu(x):
    return jax.nn.silu(x)

def _sigmoid(x):
    return jax.nn.sigmoid(x)

def _layernorm(x, axis=-1, eps=1e-05):
    m = jnp.mean(x, axis=axis, keepdims=True)
    v = jnp.var(x, axis=axis, keepdims=True)
    return (x - m) / jnp.sqrt(v + eps)

def _scatter_add(tgt, idx, src, axis=0):
    return tgt.at[idx].add(src)

def _segment_sum(src, seg, n):
    return jax.ops.segment_sum(src, seg, n)
kernel_name = 'mk_xattn_seq_d1_seqx_r4_30b351'

def setup_inputs(seed: int=0):
    np.random.seed(seed)
    _w = jnp.asarray

    def _rec_inputs():
        import jax
        import jax.numpy as jnp
        _rk = jax.random.key(seed)
        x = -0.0001233 + 1 * jax.random.normal(jax.random.fold_in(_rk, 1), (128, 128, 320), jnp.float32)
        _lenS = 128 - jax.random.randint(jax.random.fold_in(_rk, 7), (128,), 0, max(1, 128 // 4) + 1, jnp.int32)
        _lenS2 = 128 - jax.random.randint(jax.random.fold_in(_rk, 8), (128,), 0, max(1, 128 // 4) + 1, jnp.int32)
        _ctx_2048P = jax.random.normal(jax.random.fold_in(_rk, 11), (128, 16, 512), jnp.float32)
        _ctx_2048c = jax.random.dirichlet(jax.random.fold_in(_rk, 511), 0.3 * jnp.ones((16,), jnp.float32), (128, 128))
        _ctx_2048t = jnp.einsum('bsk,bkd->bsd', _ctx_2048c, _ctx_2048P)
        _ctx_2048t = _ctx_2048t * jax.lax.rsqrt(jnp.mean(jnp.square(_ctx_2048t)) + 1e-12) * 0.953939
        ctx_2048 = 0.00266749 + 0.998873 * (_ctx_2048t + 0.3 * jax.random.normal(jax.random.fold_in(_rk, 611), (128, 128, 512), jnp.float32))
        return (x, ctx_2048)
    x, ctx_2048 = _rec_inputs()

    def _L0_xattn_setup():
        import jax, jax.numpy as jnp
        import numpy as np
        B, S, C = (2, 1024, 320)
        CA = 512
        HEADS = 20
        HD = C // HEADS
        N_TXT, N_OBJ, N_OTH, N_IP = (77, 4, 4, 16)
        SCALE_OBJ = SCALE_OTH = SCALE_IP = 1.0
        RESCALE = 1.0

        def _heads(x):
            b, l, _ = x.shape
            return x.reshape(b, l, HEADS, HD).transpose(0, 2, 1, 3)

        def _merge(x):
            b, h, l, d = x.shape
            return x.transpose(0, 2, 1, 3).reshape(b, l, h * d)

        def _sdpa(q, k, v):
            scale = 1.0 / np.sqrt(HD).astype(np.float32)
            s = jnp.einsum('bhqd,bhkd->bhqk', q, k) * scale
            p = jax.nn.softmax(s, axis=-1)
            return jnp.einsum('bhqk,bhkd->bhqd', p, v)
        key = jax.random.key(seed)
        ks = jax.random.split(key, 16)
        g = lambda k, shp, fan: jax.random.normal(k, shp, jnp.float32) / np.sqrt(fan).astype(np.float32)
        return {'hidden_states': jax.random.normal(ks[0], (B, S, C), jnp.float32), 'encoder_hidden_states': jax.random.normal(ks[1], (B, N_TXT + N_OBJ + N_OTH + N_IP, CA), jnp.float32), 'to_q_w': g(ks[2], (C, C), C), 'to_k_w': g(ks[3], (CA, C), CA), 'to_v_w': g(ks[4], (CA, C), CA), 'to_k_object_w': g(ks[5], (CA, C), CA), 'to_v_object_w': g(ks[6], (CA, C), CA), 'to_k_others_w': g(ks[7], (CA, C), CA), 'to_v_others_w': g(ks[8], (CA, C), CA), 'to_k_ip_w': g(ks[9], (CA, C), CA), 'to_v_ip_w': g(ks[10], (CA, C), CA), 'to_out_w': g(ks[11], (C, C), C), 'to_out_b': jnp.zeros((C,), jnp.float32)}
    _L0_xattn_all = _L0_xattn_setup()
    _L0_xattn_in = {k: v for k, v in _L0_xattn_all.items() if k in ('to_q_w', 'to_k_w', 'to_v_w', 'to_k_object_w', 'to_v_object_w', 'to_k_others_w', 'to_v_others_w', 'to_k_ip_w', 'to_v_ip_w', 'to_out_w', 'to_out_b')}
    del _L0_xattn_all
    return {'x': x, 'ctx_2048': ctx_2048, 'L0_xattn_to_q_w': _L0_xattn_in['to_q_w'], 'L0_xattn_to_k_w': _L0_xattn_in['to_k_w'], 'L0_xattn_to_v_w': _L0_xattn_in['to_v_w'], 'L0_xattn_to_k_object_w': _L0_xattn_in['to_k_object_w'], 'L0_xattn_to_v_object_w': _L0_xattn_in['to_v_object_w'], 'L0_xattn_to_k_others_w': _L0_xattn_in['to_k_others_w'], 'L0_xattn_to_v_others_w': _L0_xattn_in['to_v_others_w'], 'L0_xattn_to_k_ip_w': _L0_xattn_in['to_k_ip_w'], 'L0_xattn_to_v_ip_w': _L0_xattn_in['to_v_ip_w'], 'L0_xattn_to_out_w': _L0_xattn_in['to_out_w'], 'L0_xattn_to_out_b': _L0_xattn_in['to_out_b']}

def reference(x, ctx_2048, L0_xattn_to_q_w, L0_xattn_to_k_w, L0_xattn_to_v_w, L0_xattn_to_k_object_w, L0_xattn_to_v_object_w, L0_xattn_to_k_others_w, L0_xattn_to_v_others_w, L0_xattn_to_k_ip_w, L0_xattn_to_v_ip_w, L0_xattn_to_out_w, L0_xattn_to_out_b):
    import jax
    import jax.numpy as jnp

    def _L0_xattn_ref(hidden_states, encoder_hidden_states, to_q_w, to_k_w, to_v_w, to_k_object_w, to_v_object_w, to_k_others_w, to_v_others_w, to_k_ip_w, to_v_ip_w, to_out_w, to_out_b):
        import jax, jax.numpy as jnp
        import numpy as np
        B, S, C = (2, 1024, 320)
        CA = 512
        HEADS = 20
        HD = C // HEADS
        N_TXT, N_OBJ, N_OTH, N_IP = (77, 4, 4, 16)
        SCALE_OBJ = SCALE_OTH = SCALE_IP = 1.0
        RESCALE = 1.0

        def _heads(x):
            b, l, _ = x.shape
            return x.reshape(b, l, HEADS, HD).transpose(0, 2, 1, 3)

        def _merge(x):
            b, h, l, d = x.shape
            return x.transpose(0, 2, 1, 3).reshape(b, l, h * d)

        def _sdpa(q, k, v):
            scale = 1.0 / np.sqrt(HD).astype(np.float32)
            s = jnp.einsum('bhqd,bhkd->bhqk', q, k) * scale
            p = jax.nn.softmax(s, axis=-1)
            return jnp.einsum('bhqk,bhkd->bhqd', p, v)
        residual = hidden_states
        end = N_TXT
        ehs_txt = encoder_hidden_states[:, :end]
        ehs_obj = encoder_hidden_states[:, end:end + N_OBJ]
        ehs_oth = encoder_hidden_states[:, end + N_OBJ:end + N_OBJ + N_OTH]
        ehs_ip = encoder_hidden_states[:, end + N_OBJ + N_OTH:]
        q = _heads(hidden_states @ to_q_w)
        h_txt = _sdpa(q, _heads(ehs_txt @ to_k_w), _heads(ehs_txt @ to_v_w))
        h_obj = _sdpa(q, _heads(ehs_obj @ to_k_object_w), _heads(ehs_obj @ to_v_object_w))
        h_oth = _sdpa(q, _heads(ehs_oth @ to_k_others_w), _heads(ehs_oth @ to_v_others_w))
        h_ip = _sdpa(q, _heads(ehs_ip @ to_k_ip_w), _heads(ehs_ip @ to_v_ip_w))
        out = _merge(h_txt) + SCALE_OBJ * _merge(h_obj) + SCALE_OTH * _merge(h_oth) + SCALE_IP * _merge(h_ip)
        out = out @ to_out_w + to_out_b
        out = (out + residual) / RESCALE
        return out
    x = _L0_xattn_ref(x, ctx_2048, L0_xattn_to_q_w, L0_xattn_to_k_w, L0_xattn_to_v_w, L0_xattn_to_k_object_w, L0_xattn_to_v_object_w, L0_xattn_to_k_others_w, L0_xattn_to_v_others_w, L0_xattn_to_k_ip_w, L0_xattn_to_v_ip_w, L0_xattn_to_out_w, L0_xattn_to_out_b)
    return x

_drawn_inputs = setup_inputs


def setup_inputs(seed=0):
    import zlib

    import numpy as np

    out = dict(_drawn_inputs(seed))
    spreads = {'L0_xattn_to_out_b': (0.0, 0.1)}
    factors = {}
    for name, (base, spread) in spreads.items():
        noise = np.random.default_rng([zlib.crc32(name.encode()), seed]).standard_normal(out[name].shape)
        drawn = base * np.exp(spread * noise) if base else spread * noise
        out[name] = jnp.asarray(drawn.astype(out[name].dtype))
    for name, factor in factors.items():
        out[name] = (out[name] * factor).astype(out[name].dtype)
    return out
```

```python
import concourse.bass as bass
from concourse import mybir
from contextlib import ExitStack

B, S, T = 128, 128, 128
C, CA = 320, 512
H = 20
D = C // H
SEGS = [(0, 77), (77, 81), (81, 85), (85, 128)]
NSEG = len(SEGS)
SCALE = 1.0 / float(D) ** 0.5

P = 128
NB = 4
G = B // NB
QH = 4
NQ = H // QH
NPAIR = NB // 2
SLOTS = 6
Q_PART = [0, 0, 0, 1, 1, 2]
K_PART = [0, 1, 2, 0, 1, 0]
KS = SLOTS * D
HM = H // 2
RM = 2 * NSEG
W = D + 1
CK = CA // P
MKV = 2 * C // P
CT = C - 2 * P

JOBS = ([("ctx", b) for b in range(NB)] + [("kv", m) for m in range(MKV)] + [("v", 0)]
        + [("x", b) for b in range(NB)] + [("q", m) for m in range(3)] + [("v", b) for b in range(1, NB)])
JOB_AT = [0] * NB + [1, 2, 3, 4, 5] + [6] + [7] * NB + [8, 9, 10] + [11, 12, 13]
NJ = len(JOBS)
SPLITS = [("kv", 0), ("kv", 1), ("kv", 2), ("q", 0), ("q", 1), ("q", 2)]
NSP = len(SPLITS)
MAX_AT = [0, 0, 1, 2, 3]


def job_no(kind, i):
    return JOBS.index((kind, i))


def jobs_at(pos):
    return [n for n in range(NJ) if JOB_AT[n] == pos]


def v_seg_pieces():
    pieces = []
    for s, (a, e) in enumerate(SEGS):
        while a < e:
            n = e - a if e - a < 16 else 16 * ((e - a) // 16)
            pieces.append((s, a, n))
            a += n
    return pieces


N_VD = len(v_seg_pieces())


def split_rows(n):
    return CT if SPLITS[n][1] == 2 else P


def xattn_kernel(nc: bass.Bass, x, ctx_in, wq, wk, wv, wko, wvo, wkt, wvt, wki, wvi, wo, bo, shift_rows, out):
    fp32 = mybir.dt.float32
    bf16 = mybir.dt.bfloat16
    ALU = mybir.AluOpType
    ACT = mybir.ActivationFunctionType
    AX = mybir.AxisListType

    q_scr = nc.dram_tensor("q_scratch", [G, 3, C, NB * S], bf16, kind="Internal").ap()
    k_scr = nc.dram_tensor("k_scratch", [G, 3, C, NB * T], bf16, kind="Internal").ap()

    with ExitStack() as stack:
        def sb(name, shape, dt=fp32):
            return stack.enter_context(nc.sbuf_tensor(name, shape, dt))

        def bank(name):
            return stack.enter_context(nc.psum_tensor(name, [P, 512], fp32))

        def sem(name):
            return stack.enter_context(nc.semaphore(name))

        x_in = sb("x_in", [P, NB, C])
        x_res = sb("x_res", [P, NB, C])
        c_in = sb("c_in", [P, NB, CA])
        xT = sb("xT", [P, 3, NB, S])
        cT = sb("cT", [P, CK, NB, T])
        vT = sb("vT", [P, 3, NB, T])
        wkv = sb("wkv", [P, NSEG, CK, 2 * C])
        wq_sb = sb("wq_sb", [P, 3, C])
        wo_sb = sb("wo_sb", [P, 3, C])
        bias = sb("bias", [P, C])
        ident = sb("ident", [P, P])
        zero = sb("zero", [P, 1])
        ident_b = sb("ident_b", [P, P], bf16)
        shift_f = sb("shift_f", [HM * RM, 2 * T])
        shift_w = sb("shift_w", [HM * RM, HM, T], bf16)
        parts = sb("parts", [P, 2, 3, NB * S], bf16)
        rest = sb("rest", [P, 2, NB * S])
        q_st = [sb(f"q_st{i}", [KS, H, 2, S], bf16) for i in range(NPAIR)]
        k_st = [sb(f"k_st{i}", [KS, H, 2, T], bf16) for i in range(NPAIR)]
        m_seg = sb("m_seg", [P, H, NSEG])
        nm = sb("nm", [P, H, 2, NSEG], bf16)
        mT = sb("mT", [HM * RM, 2, 2, S], bf16)
        pT = sb("pT", [P, 2, QH, S])
        v_new = sb("v_new", [P, NPAIR, 2, H, W])
        v_seg = [sb(f"v_seg{i}", [P, 2, NSEG, H * W]) for i in range(NPAIR)]
        rl = sb("rl", [P, QH, NSEG, 1])
        o_seg = sb("o_seg", [P, 2, NSEG, H, D])
        o_two = sb("o_two", [P, 2, C])
        o = sb("o", [P, C])
        oT = sb("oT", [P, 3, S])
        y = sb("y", [P, NPAIR, 2, C])

        max_ps = [bank(f"max_ps{i}") for i in range(2)]
        sc_ps = [bank(f"sc_ps{i}") for i in range(2)]
        pv_ps = [bank(f"pv_ps{i}") for i in range(2)]
        job_ps = bank("job_ps")
        tail_ps = bank("tail_ps")
        mT_ps = tail_ps[:, :].bitcast(bf16)

        w_loaded = sem("w_loaded")
        consts_made = sem("consts_made")
        shift_loaded = sem("shift_loaded")
        consts_cast = sem("consts_cast")
        x_loaded = sem("x_loaded")
        c_loaded = sem("c_loaded")
        job_filled = sem("job_filled")
        job_freed = sem("job_freed")
        part1_made = sem("part1_made")
        part2_made = sem("part2_made")
        part3_made = sem("part3_made")
        parts_stored = [sem(f"parts_stored{i}") for i in range(2)]
        stack_loaded = [sem(f"stack_loaded{i}") for i in range(NPAIR)]
        v_seg_loaded = [sem(f"v_seg_loaded{i}") for i in range(NPAIR)]
        max_filled = sem("max_filled")
        max_reduced = sem("max_reduced")
        nm_hi_made = sem("nm_hi_made")
        nm_made = sem("nm_made")
        mT_filled = sem("mT_filled")
        mT_copied = sem("mT_copied")
        sc_filled = sem("sc_filled")
        exp_done = sem("exp_done")
        pv_filled = sem("pv_filled")
        rl_made = sem("rl_made")
        normalised = sem("normalised")
        o_two_made = sem("o_two_made")
        o_made = sem("o_made")
        oT_filled = sem("oT_filled")
        oT_copied = sem("oT_copied")
        y_filled = sem("y_filled")
        y_made = sem("y_made")
        x_res_made = sem("x_res_made")
        v_head_copied = sem("v_head_copied")
        y_stored = [sem(f"y_stored{i}") for i in range(NPAIR)]

        block = stack.enter_context(nc.Block())

        def after(eng, s, value):
            if not isinstance(value, int) or value > 0:
                eng.wait_ge(s, value)

        def groups(eng, body):
            body(0)
            with eng.Fori(1, G - 1) as g:
                body(g)
            body(G - 1)

        def is_last(g):
            return isinstance(g, int) and g == G - 1

        seg_w = [(wk, wv), (wko, wvo), (wkt, wvt), (wki, wvi)]
        N_W = 2 * NSEG + 2 * 2 + 1

        @block.sync
        def _(sp):
            def load_c(g):
                after(sp, job_filled, g * NJ + NB - NJ if isinstance(g, int) else (g - 1) * NJ + NB)
                sp.dma_start(c_in[:, :, :], ctx_in[bass.ts(g, NB)].rearrange("b t c -> t b c")).then_inc(c_loaded, 16)

            def load_x(g):
                sp.dma_start(x_in[:, :, :], x[bass.ts(g, NB)].rearrange("b s c -> s b c")).then_inc(x_loaded, 16)

            def store_parts(g, n):
                kind, m = SPLITS[n]
                r = split_rows(n)
                scr = q_scr if kind == "q" else k_scr
                sp.wait_ge(part3_made, g * NSP + n + 1)
                sp.dma_start(scr[g, :, m * P:m * P + r, :].rearrange("a c n -> c a n"),
                             parts[0:r, n % 2, :, :]).then_inc(parts_stored[n % 2], 16)

            def load_stack(g, h):
                for i in range(2):
                    sp.wait_ge(parts_stored[i], (g + 1) * (NSP // 2) * 16)
                after(sp, sc_filled, (g * NB + 2 * h + 2 - NB) * NQ)
                for st, scr, part in ((q_st, q_scr, Q_PART), (k_st, k_scr, K_PART)):
                    for i in range(SLOTS):
                        sp.dma_start(st[h][i * D:(i + 1) * D, :, :, :].rearrange("d h b n -> d h (b n)"),
                                     scr[g, part[i], :, h * 2 * S:(h + 1) * 2 * S]
                                     .rearrange("(h d) n -> d h n", d=D)).then_inc(stack_loaded[h], 16)

            def load_v_seg(g, h):
                sp.wait_ge(job_freed, g * NJ + job_no("v", 2 * h + 1) + 1)
                after(sp, pv_filled, (g * NB + 2 * h + 2 - NB) * NQ)
                for s, a, n in v_seg_pieces():
                    sp.dma_start(v_seg[h][a:a + n, :, s, :],
                                 v_new[a:a + n, h, :, :, :].rearrange("t b h w -> t b (h w)"))\
                      .then_inc(v_seg_loaded[h], 16)

            def store_y(g, h):
                sp.wait_ge(y_made, g * NB + 2 * h + 2)
                sp.dma_start(out[bass.ds(g * NB + 2 * h, 2)].rearrange("b s c -> s b c"), y[:, h, :, :])\
                  .then_inc(y_stored[h], 16)

            for s, (k_w, v_w) in enumerate(seg_w):
                sp.dma_start(wkv[:, s, :, 0:C], k_w.rearrange("(k p) c -> p k c", p=P)).then_inc(w_loaded, 16)
                sp.dma_start(wkv[:, s, :, C:2 * C], v_w.rearrange("(k p) c -> p k c", p=P)).then_inc(w_loaded, 16)
            load_c(0)
            load_x(0)
            for w_sb, w in ((wq_sb, wq), (wo_sb, wo)):
                sp.dma_start(w_sb[:, 0:2, :], w[0:2 * P, :].rearrange("(k p) c -> p k c", p=P)).then_inc(w_loaded, 16)
                sp.dma_start(w_sb[P - CT:P, 2, :], w[2 * P:C, :]).then_inc(w_loaded, 16)
            sp.dma_start(bias[:, :], bo.rearrange("(a c) -> a c", a=1).broadcast_to((P, C))).then_inc(w_loaded, 16)
            for n in range(HM // 2):
                if n:
                    sp.wait_ge(consts_cast, n)
                sp.dma_start(shift_f[:, :], shift_rows[:, n * 2 * T:(n + 1) * 2 * T]).then_inc(shift_loaded, 16)
            for n in range(NSP):
                store_parts(0, n)
            load_stack(0, 0)
            load_c(1)
            load_v_seg(0, 0)

            def body(g):
                load_stack(g, 1)
                load_v_seg(g, 1)
                if not is_last(g):
                    for n in range(2):
                        store_parts(g + 1, n)
                if not (isinstance(g, int) and g == 0):
                    store_y(g - 1, 1)
                if not is_last(g):
                    store_parts(g + 1, 2)
                    sp.wait_ge(x_res_made, (g + 1) * NB)
                    load_x(g + 1)
                    for n in range(3, NSP):
                        store_parts(g + 1, n)
                    load_stack(g + 1, 0)
                    load_v_seg(g + 1, 0)
                    if not (isinstance(g, int) and g == G - 2):
                        load_c(g + 2)
                store_y(g, 0)

            body(0)
            with sp.Fori(1, G - 2) as g:
                body(g)
            body(G - 2)
            body(G - 1)
            store_y(G - 1, 1)
            for h in range(NPAIR):
                sp.wait_ge(y_stored[h], 16 * G)

        @block.gpsimd
        def _(pool):
            pool.memset(ident[:, :], 0.0).then_inc(consts_made, 1)
            pool.memset(ident_b[:, :], 0.0).then_inc(consts_made, 1)
            for h in range(NPAIR):
                pool.memset(v_seg[h][:, :, :, :], 0.0).then_inc(consts_made, 1)
            pool.memset(v_new[:, :, :, :, :], 1.0).then_inc(consts_made, 1)
            pool.memset(zero[:, :], 0.0).then_inc(consts_made, 1)
            pool.wait_ge(consts_made, 6)
            for m in (ident, ident_b):
                pool.affine_select(out=m[:, :], in_=m[:, :], compare_op=ALU.not_equal, fill=1.0, base=0,
                                   pattern=[[-1, P]], channel_multiplier=1).then_inc(consts_made, 1)

            def split(g, n):
                r = split_rows(n)
                kind, m = SPLITS[n]
                src, dst = rest[0:r, n % 2, :], parts[0:r, n % 2, :, :]
                pool.wait_ge(job_freed, g * NJ + job_no(kind, m) + 1)
                if n >= 2:
                    pool.wait_ge(parts_stored[n % 2], g * (NSP // 2) * 16 + 16 * (n // 2))
                else:
                    after(pool, parts_stored[n % 2], g * (NSP // 2) * 16)
                pool.tensor_tensor(dst[:, 1, :], src, zero[0:r, :].broadcast_to((r, NB * S)), ALU.add)\
                    .then_inc(part2_made, 1)
                pool.wait_ge(part2_made, g * NSP + n + 1)
                pool.tensor_tensor(dst[:, 2, :], src, dst[:, 1, :], ALU.subtract).then_inc(part3_made, 1)

            def add_bias(g, s):
                pool.wait_ge(x_loaded, (g + 1) * 16)
                after(pool, y_made, g * NB + s + 1 - NB)
                pool.tensor_tensor(x_res[:, s, :], x_in[:, s, :], bias[:, :], ALU.add).then_inc(x_res_made, 1)

            def merge(b, parity):
                pool.wait_ge(normalised, (b + 1) * NQ)
                v = o_seg[:, parity, :, :, :].rearrange("p a h d -> p a (h d)")
                pool.tensor_tensor(o_two[:, :, :], v[:, 0:2, :], v[:, 2:4, :], ALU.add).then_inc(o_two_made, 1)
                pool.wait_ge(o_two_made, b + 1)
                after(pool, oT_filled, b)
                pool.tensor_tensor(o[:, :], o_two[:, 0, :], o_two[:, 1, :], ALU.add).then_inc(o_made, 1)

            pool.wait_ge(w_loaded, 16 * N_W)
            for n in range(NSP):
                split(0, n)
            for s in range(2):
                add_bias(0, s)

            def body(g):
                for s in range(NB):
                    b = g * NB + s
                    if s == 0:
                        add_bias(g, 2)
                    if s == 1:
                        add_bias(g, 3)
                    if s >= 2 and not is_last(g):
                        add_bias(g + 1, s - 2)
                    if s or not (isinstance(g, int) and g == 0):
                        merge(b - 1, (s - 1) % 2)
                    if not is_last(g):
                        for n in range(NSP):
                            if JOB_AT[job_no(*SPLITS[n])] // NQ == s:
                                split(g + 1, n)

            groups(pool, body)
            merge(B - 1, 1)

        @block.scalar
        def _(act):
            def evacuate(g, n):
                kind, i = JOBS[n]
                act.wait_ge(job_filled, g * NJ + n + 1)
                if kind == "ctx":
                    act.activation(cT[:, :, i, :], job_ps[:, :].rearrange("p (k t) -> p k t", k=CK), ACT.Copy)\
                       .then_inc(job_freed, 1)
                elif kind == "x":
                    act.activation(xT[:, :, i, :], job_ps[:, 0:3 * S].rearrange("p (k t) -> p k t", k=3), ACT.Copy)\
                       .then_inc(job_freed, 1)
                elif kind == "v":
                    if i % 2 == 0:
                        after(act, v_seg_loaded[i // 2], g * 16 * N_VD)
                    if isinstance(g, int) and g == 0:
                        act.wait_ge(consts_made, 8)
                    act.activation(v_new[:, i // 2, i % 2, :, 0:D], job_ps[:, 0:C].rearrange("p (h d) -> p h d", d=D),
                                   ACT.Copy).then_inc(job_freed, 1)
                elif kind == "kv" and i > 2:
                    act.activation(vT[:, i - 2, :, :], job_ps[:, :].rearrange("p (b t) -> p b t", b=NB), ACT.Copy)\
                       .then_inc(job_freed, 1)
                else:
                    if (kind, i) == ("kv", 2):
                        act.activation(vT[CT:P, 0, :, :], job_ps[CT:P, :].rearrange("p (b t) -> p b t", b=NB), ACT.Copy)\
                           .then_inc(v_head_copied, 1)
                    m = SPLITS.index((kind, i))
                    r = split_rows(m)
                    if m >= 2:
                        act.wait_ge(parts_stored[m % 2], g * (NSP // 2) * 16 + 16 * (m // 2))
                    else:
                        after(act, parts_stored[m % 2], g * (NSP // 2) * 16)
                    act.activation(parts[0:r, m % 2, 0, :], job_ps[0:r, :], ACT.Copy).then_inc(part1_made, 1)

            def copy_mT(b, parity):
                act.wait_ge(mT_filled, b + 1)
                after(act, sc_filled, (b - 1) * NQ)
                act.activation(mT[:, parity, :, :], mT_ps[0:HM * RM, 0:2 * S].rearrange("p (a s) -> p a s", a=2),
                               ACT.Copy).then_inc(mT_copied, 1)

            for n in range(NJ):
                evacuate(0, n)
            copy_mT(0, 0)

            def body(g):
                for s in range(NB):
                    b = g * NB + s
                    for j in range(NQ):
                        n = b * NQ + j
                        act.wait_ge(sc_filled, n + 1)
                        after(act, pv_filled, n - 1)
                        act.activation(pT[:, (s * NQ + j) % 2, :, :],
                                       sc_ps[(s * NQ + j) % 2][:, :].rearrange("p (h s) -> p h s", h=QH),
                                       ACT.Exp, scale=SCALE).then_inc(exp_done, 1)
                        if not is_last(g):
                            for i in jobs_at(s * NQ + j):
                                evacuate(g + 1, i)
                        if j == 3 and (s or not (isinstance(g, int) and g == 0)):
                            copy_oT(b - 1)
                        if j == 4 and not (is_last(g) and s == NB - 1):
                            copy_mT(b + 1, (s + 1) % 2)

            def copy_oT(b):
                act.wait_ge(oT_filled, b + 1)
                after(act, y_filled, b)
                act.activation(oT[:, :, :], tail_ps[:, 0:3 * S].rearrange("p (k s) -> p k s", k=3), ACT.Copy)\
                   .then_inc(oT_copied, 1)

            groups(act, body)
            copy_oT(B - 1)

        @block.vector
        def _(dve):
            def reduce_max(b, j):
                dve.wait_ge(max_filled, b * NQ + j + 1)
                sc = max_ps[mod2(b, j)][:, :].rearrange("p (h t) -> p h t", h=QH)
                hs = slice(j * QH, (j + 1) * QH)
                for s, (a, e) in enumerate(SEGS):
                    last = dve.tensor_reduce(m_seg[:, hs, s:s + 1], sc[:, :, a:e], axis=AX.X, op=ALU.max)
                last.then_inc(max_reduced, 1)

            def mod2(b, j):
                return (place[0] * NQ + j) % 2

            place = [0]

            def negate(b):
                dve.wait_ge(max_reduced, (b + 1) * NQ)
                after(dve, mT_filled, b)
                dve.tensor_scalar(nm[:, :, 0, :], m_seg[:, :, :], -1.0, None, ALU.mult).then_inc(nm_hi_made, 1)
                dve.wait_ge(nm_hi_made, b + 1)
                dve.scalar_tensor_tensor(out=nm[:, :, 1, :], in0=m_seg[:, :, :], scalar=-1.0, in1=nm[:, :, 0, :],
                                         op0=ALU.mult, op1=ALU.subtract).then_inc(nm_made, 1)

            def subtract_part(g, n):
                kind, m = SPLITS[n]
                r = split_rows(n)
                dve.wait_ge(part1_made, g * NSP + n + 1)
                after(dve, part3_made, g * NSP + n - 1)
                dve.tensor_tensor(rest[0:r, n % 2, :], job_ps[0:r, :], parts[0:r, n % 2, 0, :], ALU.subtract)\
                   .then_inc(job_freed, 1)

            def normalise(n, i, s, j):
                dve.wait_ge(pv_filled, n + 1)
                pv = pv_ps[i][:, 0:QH * NSEG * W].rearrange("p (h a w) -> p h a w", h=QH, a=NSEG)
                after(dve, normalised, n)
                dve.reciprocal(rl[:, :, :, :], pv[:, :, :, D:W]).then_inc(rl_made, 1)
                dve.wait_ge(rl_made, n + 1)
                if j == 0:
                    after(dve, o_two_made, (n - NQ) // NQ if isinstance(n, int) else merged_before[0])
                dve.tensor_tensor(o_seg[:, s % 2, :, j * QH:(j + 1) * QH, :].rearrange("p a h d -> p h a d"),
                                  pv[:, :, :, 0:D], rl[:, :, :, :].broadcast_to((P, QH, NSEG, D)), ALU.mult)\
                   .then_inc(normalised, 1)

            merged_before = [0]

            def add_residual(g, s, b):
                dve.wait_ge(y_filled, b + 1)
                dve.wait_ge(x_res_made, b + 1)
                if s % 2 == 0:
                    after(dve, y_stored[s // 2], g * 16)
                dve.tensor_tensor(y[:, s // 2, s % 2, :], tail_ps[:, 0:C], x_res[:, s, :], ALU.add).then_inc(y_made, 1)

            for n in range(HM // 2):
                dve.wait_ge(shift_loaded, 16 * (n + 1))
                dve.tensor_copy(shift_w[:, 2 * n:2 * n + 2, :], shift_f[:, :].rearrange("p (h t) -> p h t", h=2))\
                   .then_inc(consts_cast, 1)
            for n in range(NSP):
                subtract_part(0, n)
            place[0] = 0
            for j in range(NQ):
                reduce_max(0, j)
            negate(0)

            def body(g):
                for s in range(NB):
                    b = g * NB + s
                    for j in range(NQ):
                        place[0] = s + 1
                        nxt = not (is_last(g) and s == NB - 1)
                        if nxt:
                            for jj in range(NQ):
                                if MAX_AT[jj] == j:
                                    reduce_max(b + 1, jj)
                            if MAX_AT[NQ - 1] == j:
                                negate(b + 1)
                        if not is_last(g):
                            for i in jobs_at(s * NQ + j):
                                if JOBS[i] in SPLITS:
                                    subtract_part(g + 1, SPLITS.index(JOBS[i]))
                        if s or j or not (isinstance(g, int) and g == 0):
                            q = s * NQ + j - 1
                            merged_before[0] = b - 1
                            ss, jj = divmod(q % (NB * NQ), NQ)
                            normalise(b * NQ + j - 1, q % 2, ss, jj)
                        if j == 4 and (s or not (isinstance(g, int) and g == 0)):
                            pg = g if s else g - 1
                            add_residual(pg, (s - 1) % NB, b - 1)

            groups(dve, body)
            normalise(B * NQ - 1, 1, NB - 1, NQ - 1)
            add_residual(G - 1, NB - 1, B - 1)

        @block.tensor
        def _(pe):
            def job(g, n):
                kind, i = JOBS[n]
                after(pe, job_freed, g * NJ + n)
                if kind == "ctx":
                    if i == 0:
                        pe.wait_ge(c_loaded, (g + 1) * 16)
                    for k in range(CK):
                        last = pe.transpose(job_ps[:, k * T:(k + 1) * T], c_in[:, i, k * P:(k + 1) * P], ident[:, :])
                elif kind == "x":
                    if i == 0:
                        pe.wait_ge(x_loaded, (g + 1) * 16)
                    for k, at in enumerate((0, P, C - P)):
                        last = pe.transpose(job_ps[:, k * S:(k + 1) * S], x_in[:, i, at:at + P], ident[:, :])
                elif kind == "kv":
                    ps = job_ps[:, :].rearrange("p (b t) -> p b t", b=NB)
                    for s, (a, e) in enumerate(SEGS):
                        for k in range(CK):
                            last = pe.matmul(ps[:, :, a:e], wkv[:, s, k, i * P:(i + 1) * P], cT[:, k, :, a:e],
                                             start=(k == 0), stop=(k == CK - 1))
                elif kind == "q":
                    r = CT if i == 2 else P
                    for k in range(3):
                        f = P - CT if k == 2 else 0
                        last = pe.matmul(job_ps[0:r, :], wq_sb[f:P, k, i * P:i * P + r],
                                         xT[f:P, k, :, :].rearrange("p b s -> p (b s)"), start=(k == 0), stop=(k == 2))
                else:
                    for k in range(1, 3):
                        pe.transpose(job_ps[:, CT + (k - 1) * P:CT + k * P], vT[:, k, i, :], ident[:, :])
                    last = pe.transpose(job_ps[:, 0:CT], vT[CT:P, 0, i, :], ident[CT:P, CT:P])
                last.then_inc(job_filled, 1)

            def max_scores(g, s, b, j):
                i = (s * NQ + j) % 2
                if j == 0 and s % 2 == 0:
                    pe.wait_ge(stack_loaded[s // 2], (g + 1) * 16 * 2 * SLOTS)
                after(pe, max_reduced, b * NQ + j - 1)
                for h in range(QH):
                    hh = j * QH + h
                    last = pe.matmul(max_ps[i][:, h * T:(h + 1) * T], q_st[s // 2][:, hh, s % 2, :],
                                     k_st[s // 2][:, hh, s % 2, :], start=True, stop=True)
                last.then_inc(max_filled, 1)

            def transpose_shifts(b):
                pe.wait_ge(nm_made, b + 1)
                after(pe, y_made, b - 1)
                v = nm[:, :, :, :].rearrange("p (a h) r s -> p a (h r s)", a=2)
                for a in range(2):
                    last = pe.transpose(mT_ps[0:HM * RM, a * S:(a + 1) * S], v[:, a, :], ident_b[:, :])
                last.then_inc(mT_filled, 1)

            def scores(s, b, j):
                i = (s * NQ + j) % 2
                if j == 0:
                    pe.wait_ge(mT_copied, b + 1)
                after(pe, exp_done, b * NQ + j - 1)
                for h in range(QH):
                    hh = j * QH + h
                    dst = sc_ps[i][:, h * S:(h + 1) * S]
                    pe.matmul(dst, k_st[s // 2][:, hh, s % 2, :], q_st[s // 2][:, hh, s % 2, :], start=True, stop=False)
                    last = pe.matmul(dst, shift_w[:, hh % HM, :], mT[:, s % 2, hh // HM, :], start=False, stop=True)
                last.then_inc(sc_filled, 1)

            def values(g, s, j, n):
                i = (s * NQ + j) % 2
                pe.wait_ge(exp_done, n + 1)
                if j == 0 and s % 2 == 0:
                    pe.wait_ge(v_seg_loaded[s // 2], (g + 1) * 16 * N_VD)
                after(pe, normalised, n - 1)
                for h in range(QH):
                    hh = j * QH + h
                    last = pe.matmul(pv_ps[i][:, h * NSEG * W:(h + 1) * NSEG * W], pT[:, i, h, :],
                                     v_seg[s // 2][:, s % 2, :, hh * W:(hh + 1) * W], start=True, stop=True)
                last.then_inc(pv_filled, 1)

            def transpose_o(b, shifts_done):
                pe.wait_ge(o_made, b + 1)
                pe.wait_ge(mT_copied, shifts_done)
                for k, at in enumerate((0, P, C - P)):
                    last = pe.transpose(tail_ps[:, k * S:(k + 1) * S], o[:, at:at + P], ident[:, :])
                last.then_inc(oT_filled, 1)

            def project(b):
                pe.wait_ge(oT_copied, b + 1)
                for k in range(3):
                    f = P - CT if k == 2 else 0
                    last = pe.matmul(tail_ps[:, 0:C], oT[f:P, k, :], wo_sb[f:P, k, :], start=(k == 0), stop=(k == 2))
                last.then_inc(y_filled, 1)

            pe.wait_ge(w_loaded, 16 * N_W)
            pe.wait_ge(consts_made, 8)
            pe.wait_ge(consts_cast, HM // 2)
            for n in range(NJ):
                job(0, n)
            for j in range(NQ):
                max_scores(0, 0, 0, j)
            transpose_shifts(0)

            def body(g):
                for s in range(NB):
                    b = g * NB + s
                    begun = s or not (isinstance(g, int) and g == 0)
                    for j in range(NQ):
                        if not (is_last(g) and s == NB - 1):
                            for jj in range(NQ):
                                if MAX_AT[jj] == j:
                                    max_scores(g if s < NB - 1 else g + 1, (s + 1) % NB, b + 1, jj)
                        scores(s, b, j)
                        if not is_last(g):
                            for i in jobs_at(s * NQ + j):
                                job(g + 1, i)
                        if j:
                            values(g, s, j - 1, b * NQ + j - 1)
                        elif begun:
                            values(g if s else g - 1, (s - 1) % NB, NQ - 1, b * NQ - 1)
                        if j == 3 and begun:
                            transpose_o(b - 1, b + 1)
                        if j == 4:
                            if begun:
                                project(b - 1)
                            if not (is_last(g) and s == NB - 1):
                                transpose_shifts(b + 1)

            groups(pe, body)
            values(G - 1, NB - 1, NQ - 1, B * NQ - 1)
            transpose_o(B - 1, B)
            project(B - 1)


_X = "L0_xattn_"
_INS = ["x", "ctx_2048"] + [_X + n for n in (
    "to_q_w", "to_k_w", "to_v_w", "to_k_object_w", "to_v_object_w", "to_k_others_w", "to_v_others_w",
    "to_k_ip_w", "to_v_ip_w", "to_out_w", "to_out_b")]


def kernel(**inputs):
    import numpy as _np
    import concourse.bacc as _bacc
    from concourse import mybir as _mybir
    from concourse.bass_utils import run_bass_kernel_spmd as _run

    nc = _bacc.Bacc("TRN2", target_bir_lowering=False, num_devices=1)
    arrays, args = {}, []
    for name in _INS:
        a = _np.ascontiguousarray(inputs[name])
        arrays[f"in_{name}"] = a
        args.append(nc.dram_tensor(f"in_{name}", a.shape, _mybir.dt.from_np(a.dtype), kind="ExternalInput").ap())
    rows = _np.zeros((HM, 2, NSEG, HM, T), _np.float32)
    for h in range(HM):
        for s, (a, e) in enumerate(SEGS):
            rows[h, :, s, h, a:e] = 1.0
    arrays["in_shift_rows"] = rows.reshape(HM * RM, HM * T)
    args.append(nc.dram_tensor("in_shift_rows", (HM * RM, HM * T), _mybir.dt.float32, kind="ExternalInput").ap())
    args.append(nc.dram_tensor("out_0", (B, S, C), _mybir.dt.float32, kind="ExternalOutput").ap())
    xattn_kernel(nc, *args)
    r = _run(nc, [arrays], core_ids=[0])
    return r.results[0]["out_0"]
```

```python
import concourse.bass as bass
from concourse import mybir
from contextlib import ExitStack

B, S, T = 128, 128, 128
C, CA = 320, 512
H = 20
D = C // H
SEGS = [(0, 77), (77, 81), (81, 85), (85, 128)]
NSEG = len(SEGS)
SCALE = 1.0 / float(D) ** 0.5

P = 128
NB = 4
G = B // NB
QH = 4
NQ = H // QH
NPAIR = NB // 2
SLOTS = 6
Q_PART = [0, 0, 0, 1, 1, 2]
K_PART = [0, 1, 2, 0, 1, 0]
KS = SLOTS * D
HM = H // 2
WS = 24
RM = 2 * NSEG
W = D + 1
CK = CA // P
MKV = 2 * C // P
CT = C - 2 * P

SMALL = [1, 2]
LARGE = [0, 3]
SA, SE = SEGS[SMALL[0]][0], SEGS[SMALL[-1]][1]
NSM = SE - SA
WIDE = {0: (0, SA + SA % 2), 3: (SE - SE % 2, T)}

JOBS = ([("ctx", b) for b in range(NB)] + [("kv", m) for m in range(MKV)] + [("x", b) for b in range(NB)]
        + [("q", m) for m in range(3)] + [("v", b) for b in range(NB)])
JOB_AT = [33, 35, 37, 39] + [1, 3, 5, 7, 9] + [10, 11, 12, 13] + [15, 17, 19] + [21, 23, 25, 27]
EARLY = NB
NJ = len(JOBS)
SMALL_JOBS = len(SMALL) * (NB + MKV)
SPLITS = [("kv", 0), ("kv", 1), ("kv", 2), ("q", 0), ("q", 1), ("q", 2)]
NSP = len(SPLITS)
OT_AT, Y_AT, MT_AT = 2, 3, 4
MAX_AT = [0, 0, 1, 2, 3]


def job_no(kind, i):
    return JOBS.index((kind, i))


def jobs_at(g, pos, half):
    found = [(g + 2 if n < EARLY else g + 1, n) for n in range(NJ) if JOB_AT[n] == 2 * pos + half]
    return [(gg, n) for gg, n in found if not isinstance(gg, int) or gg < G]


def jobs_before(g, n):
    return SMALL_JOBS + g * NJ + n


def v_seg_pieces():
    pieces = []
    for s, (a, e) in enumerate(SEGS):
        while a < e:
            n = e - a if e - a < 16 else 16 * ((e - a) // 16)
            pieces.append((s, a, n))
            a += n
    return pieces


N_VD = len(v_seg_pieces())
VR = (H - 1) * W + WS + 1


def split_rows(n):
    return CT if SPLITS[n][1] == 2 else P


def xattn_kernel(nc: bass.Bass, x, ctx_in, wq, wk, wv, wko, wvo, wkt, wvt, wki, wvi, wo, bo, shift_rows, out):
    fp32 = mybir.dt.float32
    fp32r = mybir.dt.float32r
    bf16 = mybir.dt.bfloat16
    ALU = mybir.AluOpType
    ACT = mybir.ActivationFunctionType
    AX = mybir.AxisListType

    q_scr = nc.dram_tensor("q_scratch", [G, 3, C, NB * S], bf16, kind="Internal").ap()
    k_scr = nc.dram_tensor("k_scratch", [G, 3, C, NB * T], bf16, kind="Internal").ap()

    small_scr = nc.dram_tensor("small_scratch", [G, P, MKV * NB * NSM], fp32, kind="Internal").ap()

    with ExitStack() as stack:
        def sb(name, shape, dt=fp32):
            return stack.enter_context(nc.sbuf_tensor(name, shape, dt))

        def bank(name):
            return stack.enter_context(nc.psum_tensor(name, [P, 512], fp32))

        def sem(name):
            return stack.enter_context(nc.semaphore(name))

        x_in = sb("x_in", [P, NB, C])
        x_res = sb("x_res", [P, NB, C])
        c_in = sb("c_in", [P, NB, CA])
        aT = [sb(f"aT{i}", [P, CK, NB, S], fp32r) for i in range(2)]
        vT = sb("vT", [P, 3, NB, T])
        w_kv = [sb(f"w_kv{i}", [P, len(LARGE), CK, 2 * C], fp32r) for i in range(2)]
        w_q = [sb(f"w_q{i}", [P, 3, 3 * P], fp32r) for i in range(2)]
        w_o = [sb(f"w_o{i}", [P, 3, C], fp32r) for i in range(2)]
        small = sb("small", [P, MKV, NB, NSM])
        bias = sb("bias", [P, C])
        ident = sb("ident", [P, P])
        zero = sb("zero", [P, 1])
        ident_b = sb("ident_b", [P, P], bf16)
        shift_w = sb("shift_w", [P, HM, T], bf16)
        parts = sb("parts", [P, 2, 3, NB * S], bf16)
        rest = sb("rest", [P, 2, NB * S])
        shift_f = rest[0:HM * RM, 0, 0:2 * T]
        q_all = sb("q_all", [P, NPAIR * H * 2 * S], bf16)
        k_all = sb("k_all", [P, NPAIR * H * 2 * T], bf16)
        q_st, k_st = ([t[:, i * H * 2 * S:(i + 1) * H * 2 * S].rearrange("p (h b n) -> p h b n", h=H, b=2)
                       for i in range(NPAIR)] for t in (q_all, k_all))
        m_seg = sb("m_seg", [P, H, NSEG])
        nm = sb("nm", [P, H, 2, NSEG], bf16)
        mT = sb("mT", [P, 2, 2, S], bf16)
        pT = sb("pT", [P, 2, QH, S])
        v_new = sb("v_new", [P, NPAIR, 2, H, W])
        v_all = sb("v_all", [P, NPAIR * 2 * NSEG * VR])
        v_seg = [v_all[:, i * 2 * NSEG * VR:(i + 1) * 2 * NSEG * VR]
                 .rearrange("p (b a w) -> p b a w", b=2, a=NSEG) for i in range(NPAIR)]
        rl = sb("rl", [P, QH, NSEG, 1])
        o_seg = sb("o_seg", [P, 2, NSEG, H, D])
        o_two = sb("o_two", [P, 2, C])
        o = sb("o", [P, C])
        oT = [sb(f"oT{i}", [P, 3, S], fp32r) for i in range(2)]
        y = sb("y", [P, 2, C])

        w_small = q_all[:, :].bitcast(fp32).rearrange("p (s k c) -> p s k c", s=len(SMALL), k=CK)
        w_large = k_all[:, :].bitcast(fp32).rearrange("p (s k c) -> p s k c", s=len(LARGE), k=CK)
        wq_raw = v_all[:, 0:3 * C].rearrange("p (k c) -> p k c", k=3)
        wo_raw = v_all[:, 3 * C:6 * C].rearrange("p (k c) -> p k c", k=3)
        small_all = v_all[:, 0:G * MKV * NB * NSM].rearrange("p (g m b t) -> p g m b t", g=G, m=MKV, b=NB)
        o_seg_flat = o_seg[:, :, :, :, :].rearrange("p b a h d -> p (b a h d)")
        cT_small = o_seg_flat[:, 0:CK * NB * P].rearrange("p (k t b) -> p k t b", k=CK, t=NB)

        max_ps = [bank(f"max_ps{i}") for i in range(2)]
        sc_ps = [bank(f"sc_ps{i}") for i in range(2)]
        pv_ps = [bank(f"pv_ps{i}") for i in range(2)]
        job_ps = bank("job_ps")
        tail_ps = bank("tail_ps")
        mT_ps = max_ps[1][:, :].bitcast(bf16)

        w_loaded = sem("w_loaded")
        consts_made = sem("consts_made")
        shift_loaded = sem("shift_loaded")
        consts_cast = sem("consts_cast")
        x_loaded = sem("x_loaded")
        c_loaded = sem("c_loaded")
        w_hi_made = sem("w_hi_made")
        w_lo_made = sem("w_lo_made")
        hi_made = sem("hi_made")
        oT_hi_made = sem("oT_hi_made")
        small_stored = sem("small_stored")
        small_loaded = sem("small_loaded")
        pads_made = sem("pads_made")
        v_cleared = sem("v_cleared")
        job_filled = sem("job_filled")
        job_freed = sem("job_freed")
        part1_made = sem("part1_made")
        part2_made = sem("part2_made")
        part3_made = sem("part3_made")
        parts_stored = [sem(f"parts_stored{i}") for i in range(2)]
        stack_loaded = [sem(f"stack_loaded{i}") for i in range(NPAIR)]
        v_seg_loaded = [sem(f"v_seg_loaded{i}") for i in range(NPAIR)]
        max_filled = sem("max_filled")
        max_reduced = sem("max_reduced")
        nm_hi_made = sem("nm_hi_made")
        nm_made = sem("nm_made")
        mT_filled = sem("mT_filled")
        mT_copied = sem("mT_copied")
        sc_filled = sem("sc_filled")
        exp_done = sem("exp_done")
        pv_filled = sem("pv_filled")
        rl_made = sem("rl_made")
        normalised = sem("normalised")
        o_two_made = sem("o_two_made")
        o_made = sem("o_made")
        oT_filled = sem("oT_filled")
        oT_copied = sem("oT_copied")
        y_filled = sem("y_filled")
        y_made = sem("y_made")
        x_res_made = sem("x_res_made")
        v_head_copied = sem("v_head_copied")
        y_stored = [sem(f"y_stored{i}") for i in range(2)]

        block = stack.enter_context(nc.Block())

        def after(eng, s, value):
            if not isinstance(value, int) or value > 0:
                eng.wait_ge(s, value)

        def groups(eng, body):
            body(0)
            with eng.Fori(1, G - 2) as g:
                body(g)
            body(G - 2)
            body(G - 1)

        def is_last(g):
            return isinstance(g, int) and g == G - 1

        FIRST_JOBS = [(0, n) for n in range(NJ)] + [(1, n) for n in range(EARLY)]
        seg_w = [(wk, wv), (wko, wvo), (wkt, wvt), (wki, wvi)]
        N_W = 2 * NSEG + 2 * 2 + 1
        W_SPLITS = [(w_large, [t[:, :, :, :] for t in w_kv]),
                    (wq_raw[:, 0:2, :], [t[:, 0:2, 0:C] for t in w_q]),
                    (wq_raw[P - CT:P, 2, :], [t[P - CT:P, 2, 0:C] for t in w_q]),
                    (wo_raw[:, 0:2, :], [t[:, 0:2, :] for t in w_o]),
                    (wo_raw[P - CT:P, 2, :], [t[P - CT:P, 2, :] for t in w_o])]

        @block.sync
        def _(sp):
            def load_c(g):
                sp.wait_ge(job_filled, SMALL_JOBS - MKV if isinstance(g, int) and g == 0 else jobs_before(g - 1, NB))
                sp.dma_start(c_in[:, :, :], ctx_in[bass.ts(g, NB)].rearrange("b t c -> t b c")).then_inc(c_loaded, 16)

            def load_small(g):
                if not (isinstance(g, int) and g == 0):
                    sp.wait_ge(job_filled, jobs_before(g - 1, NB + MKV))
                sp.dma_start(small[:, :, :, :].rearrange("p m b t -> p (m b t)"), small_scr[g]).then_inc(small_loaded, 16)

            def load_x(g):
                sp.dma_start(x_in[:, :, :], x[bass.ts(g, NB)].rearrange("b s c -> s b c")).then_inc(x_loaded, 16)

            def store_parts(g, n):
                kind, m = SPLITS[n]
                r = split_rows(n)
                scr = q_scr if kind == "q" else k_scr
                sp.wait_ge(part3_made, g * NSP + n + 1)
                sp.dma_start(scr[g, :, m * P:m * P + r, :].rearrange("a c n -> c a n"),
                             parts[0:r, n % 2, :, :]).then_inc(parts_stored[n % 2], 16)

            def load_stack(g, h, st, scr, part, stored):
                for i in range(2):
                    sp.wait_ge(parts_stored[i], (g * (NSP // 2) + (stored - i + 1) // 2) * 16)
                after(sp, sc_filled, (g * NB + 2 * h + 2 - NB) * NQ)
                for i in range(SLOTS):
                    sp.dma_start(st[h][i * D:(i + 1) * D, :, :, :].rearrange("d h b n -> d h (b n)"),
                                 scr[g, part[i], :, h * 2 * S:(h + 1) * 2 * S]
                                 .rearrange("(h d) n -> d h n", d=D)).then_inc(stack_loaded[h], 16)

            def load_k(g, h):
                load_stack(g, h, k_st, k_scr, K_PART, 3)

            def load_q(g, h):
                load_stack(g, h, q_st, q_scr, Q_PART, NSP)

            def load_v_seg(g, h):
                sp.wait_ge(v_cleared, 1)
                sp.wait_ge(job_freed, jobs_before(g, job_no("v", 2 * h + 1) + 1))
                after(sp, pv_filled, (g * NB + 2 * h + 2 - NB) * NQ)
                for s, a, n in v_seg_pieces():
                    sp.dma_start(v_seg[h][a:a + n, :, s, 0:H * W],
                                 v_new[a:a + n, h, :, :, :].rearrange("t b h w -> t b (h w)"))\
                      .then_inc(v_seg_loaded[h], 16)

            def store_y(b, parity):
                sp.wait_ge(y_made, b + 1)
                sp.dma_start(out[b], y[:, parity, :]).then_inc(y_stored[parity], 16)

            def load_small_c(i):
                a, e = SEGS[SMALL[i]]
                after(sp, job_filled, i * (NB + MKV) - MKV)
                sp.dma_start(c_in[:, :, :], ctx_in[:, a:e, :]).then_inc(c_loaded, 16)

            def load_w(w_raw, segs):
                for i, s in enumerate(segs):
                    for at, w in zip((0, C), seg_w[s]):
                        sp.dma_start(w_raw[:, i, :, at:at + C], w.rearrange("(k p) c -> p k c", p=P)).then_inc(w_loaded, 16)

            load_small_c(0)
            load_w(w_small, SMALL)
            load_w(w_large, LARGE)
            for w_sb, w in ((wq_raw, wq), (wo_raw, wo)):
                sp.dma_start(w_sb[:, 0:2, :], w[0:2 * P, :].rearrange("(k p) c -> p k c", p=P)).then_inc(w_loaded, 16)
                sp.dma_start(w_sb[P - CT:P, 2, :], w[2 * P:C, :]).then_inc(w_loaded, 16)
            sp.dma_start(bias[:, :], bo.rearrange("(a c) -> a c", a=1).broadcast_to((P, C))).then_inc(w_loaded, 16)
            load_x(0)
            for n in range(HM // 2):
                after(sp, consts_cast, n)
                sp.dma_start(shift_f, shift_rows[:, n * 2 * T:(n + 1) * 2 * T]).then_inc(shift_loaded, 16)
            load_small_c(1)
            load_c(0)
            sp.wait_ge(job_freed, SMALL_JOBS)
            sp.dma_start(small_scr.rearrange("g p n -> p g n"),
                         small_all.rearrange("p g m b t -> p g (m b t)")).then_inc(small_stored, 16)
            sp.wait_ge(small_stored, 16)
            load_small(0)
            for n in range(3):
                store_parts(0, n)
            load_c(1)
            load_k(0, 0)
            for n in range(3, NSP):
                store_parts(0, n)
            load_q(0, 0)
            load_small(1)
            load_v_seg(0, 0)

            def body(g):
                begun = not (isinstance(g, int) and g == 0)
                more = not is_last(g)
                load_k(g, 1)
                load_q(g, 1)
                load_v_seg(g, 1)
                if not (isinstance(g, int) and g >= G - 2):
                    load_c(g + 2)
                if begun:
                    store_y(g * NB - 2, 0)
                if more:
                    for n in range(2):
                        store_parts(g + 1, n)
                if begun:
                    store_y(g * NB - 1, 1)
                if more:
                    store_parts(g + 1, 2)
                    sp.wait_ge(x_res_made, (g + 1) * NB)
                    load_x(g + 1)
                    if not (isinstance(g, int) and g == G - 2):
                        load_small(g + 2)
                store_y(g * NB, 0)
                if more:
                    for n in range(3, NSP):
                        store_parts(g + 1, n)
                    load_k(g + 1, 0)
                    load_q(g + 1, 0)
                store_y(g * NB + 1, 1)
                if more:
                    load_v_seg(g + 1, 0)

            body(0)
            with sp.Fori(1, G - 2) as g:
                body(g)
            body(G - 2)
            body(G - 1)
            store_y(B - 2, 0)
            store_y(B - 1, 1)
            for i in range(2):
                sp.wait_ge(y_stored[i], 16 * B // 2)

        @block.gpsimd
        def _(pool):
            pool.memset(ident[:, :], 0.0).then_inc(consts_made, 1)
            pool.memset(ident_b[:, :], 0.0).then_inc(consts_made, 1)
            for t in w_q:
                pool.memset(t[:, :, C:3 * P].bitcast(fp32), 0.0).then_inc(consts_made, 1)
            pool.memset(v_new[:, :, :, :, :], 1.0).then_inc(consts_made, 1)
            pool.memset(zero[:, :], 0.0).then_inc(consts_made, 1)
            pool.memset(mT[:, :, :, :], 0.0).then_inc(consts_made, 1)
            pool.memset(shift_w[:, :, :], 0.0).then_inc(consts_made, 1)
            pool.wait_ge(consts_made, 8)
            for m in (ident, ident_b):
                pool.affine_select(out=m[:, :], in_=m[:, :], compare_op=ALU.not_equal, fill=1.0, base=0,
                                   pattern=[[-1, P]], channel_multiplier=1).then_inc(consts_made, 1)

            def split(g, n):
                r = split_rows(n)
                kind, m = SPLITS[n]
                src, dst = rest[0:r, n % 2, :], parts[0:r, n % 2, :, :]
                pool.wait_ge(job_freed, jobs_before(g, job_no(kind, m) + 1))
                if n >= 2:
                    pool.wait_ge(parts_stored[n % 2], g * (NSP // 2) * 16 + 16 * (n // 2))
                else:
                    after(pool, parts_stored[n % 2], g * (NSP // 2) * 16)
                pool.tensor_tensor(dst[:, 1, :], src, zero[0:r, :].broadcast_to((r, NB * S)), ALU.add)\
                    .then_inc(part2_made, 1)
                pool.wait_ge(part2_made, g * NSP + n + 1)
                pool.tensor_tensor(dst[:, 2, :], src, dst[:, 1, :], ALU.subtract).then_inc(part3_made, 1)

            def add_bias(g, s):
                pool.wait_ge(x_loaded, (g + 1) * 16)
                after(pool, y_made, g * NB + s + 1 - NB)
                pool.tensor_tensor(x_res[:, s, :], x_in[:, s, :], bias[:, :], ALU.add).then_inc(x_res_made, 1)

            def merge(b, parity):
                pool.wait_ge(normalised, (b + 1) * NQ)
                v = o_seg[:, parity, :, :, :].rearrange("p a h d -> p a (h d)")
                pool.tensor_tensor(o_two[:, :, :], v[:, 0:2, :], v[:, 2:4, :], ALU.add).then_inc(o_two_made, 1)
                pool.wait_ge(o_two_made, b + 1)
                after(pool, oT_filled, b)
                pool.tensor_tensor(o[:, :], o_two[:, 0, :], o_two[:, 1, :], ALU.add).then_inc(o_made, 1)

            pool.wait_ge(job_filled, SMALL_JOBS)
            pool.wait_ge(w_lo_made, len(W_SPLITS))
            for i, t in enumerate((q_all, k_all)):
                pool.memset(t[KS:P, :], 0.0).then_inc(pads_made, 1)
                pool.wait_ge(pads_made, i + 1)
            pool.wait_ge(small_stored, 16)
            pool.memset(v_all[:, :], 0.0).then_inc(v_cleared, 1)
            pool.wait_ge(w_loaded, 16 * N_W)
            for n in range(NSP):
                split(0, n)
            for s in range(2):
                add_bias(0, s)

            def body(g):
                for s in range(NB):
                    b = g * NB + s
                    if s == 0:
                        add_bias(g, 2)
                    if s == 1:
                        add_bias(g, 3)
                    if s >= 2 and not is_last(g):
                        add_bias(g + 1, s - 2)
                    if s or not (isinstance(g, int) and g == 0):
                        merge(b - 1, (s - 1) % 2)
                    if not is_last(g):
                        for n in range(NSP):
                            if JOB_AT[job_no(*SPLITS[n])] // (2 * NQ) == s:
                                split(g + 1, n)

            groups(pool, body)
            merge(B - 1, 1)

        @block.scalar
        def _(act):
            def evacuate(g, n):
                kind, i = JOBS[n]
                act.wait_ge(job_filled, jobs_before(g, n + 1))
                if kind == "ctx":
                    act.activation(aT[0][:, :, i, :], job_ps[:, :].rearrange("p (k t) -> p k t", k=CK), ACT.Copy)\
                       .then_inc(hi_made, 1)
                elif kind == "x":
                    act.activation(aT[0][:, 0:3, i, :], job_ps[:, 0:3 * S].rearrange("p (k t) -> p k t", k=3), ACT.Copy)\
                       .then_inc(hi_made, 1)
                elif kind == "v":
                    if i % 2 == 0:
                        after(act, v_seg_loaded[i // 2], g * 16 * N_VD)
                    if isinstance(g, int) and g == 0:
                        act.wait_ge(consts_made, 10)
                    act.activation(v_new[:, i // 2, i % 2, :, 0:D], job_ps[:, 0:C].rearrange("p (h d) -> p h d", d=D),
                                   ACT.Copy).then_inc(job_freed, 1)
                elif kind == "kv" and i > 2:
                    act.activation(vT[:, i - 2, :, :], job_ps[:, :].rearrange("p (b t) -> p b t", b=NB), ACT.Copy)\
                       .then_inc(job_freed, 1)
                else:
                    if (kind, i) == ("kv", 2):
                        act.activation(vT[CT:P, 0, :, :], job_ps[CT:P, :].rearrange("p (b t) -> p b t", b=NB), ACT.Copy)\
                           .then_inc(v_head_copied, 1)
                    m = SPLITS.index((kind, i))
                    r = split_rows(m)
                    if m >= 2:
                        act.wait_ge(parts_stored[m % 2], g * (NSP // 2) * 16 + 16 * (m // 2))
                    else:
                        after(act, parts_stored[m % 2], g * (NSP // 2) * 16)
                    act.activation(parts[0:r, m % 2, 0, :], job_ps[0:r, :], ACT.Copy).then_inc(part1_made, 1)

            def copy_mT(b, parity):
                act.wait_ge(mT_filled, b + 1)
                after(act, sc_filled, (b - 1) * NQ)
                act.activation(mT[0:HM * RM, parity, :, :], mT_ps[0:HM * RM, 0:2 * S].rearrange("p (a s) -> p a s", a=2),
                               ACT.Copy).then_inc(mT_copied, 1)

            act.wait_ge(consts_made, 10)
            act.wait_ge(w_loaded, 16 * N_W)
            for raw, w_parts in W_SPLITS:
                act.activation(w_parts[0], raw, ACT.Copy).then_inc(w_hi_made, 1)
            for i in range(len(SMALL)):
                for n in range(NB + MKV):
                    act.wait_ge(job_filled, i * (NB + MKV) + n + 1)
                    if n < NB:
                        act.activation(cT_small[:, :, n, :], job_ps[:, :].rearrange("p (k b) -> p k b", k=CK), ACT.Copy)\
                           .then_inc(job_freed, 1)
                    else:
                        act.wait_ge(w_lo_made, len(W_SPLITS))
                        k = SEGS[SMALL[i]][0] - SA
                        act.activation(small_all[:, :, n - NB, :, k:k + NB].rearrange("p g b t -> p t g b"),
                                       job_ps[:, :].rearrange("p (t g b) -> p t g b", t=NB, g=G), ACT.Copy)\
                           .then_inc(job_freed, 1)
            for g, n in FIRST_JOBS:
                evacuate(g, n)
            copy_mT(0, 0)

            def body(g):
                for s in range(NB):
                    b = g * NB + s
                    for j in range(NQ):
                        if j == MT_AT and not (is_last(g) and s == NB - 1):
                            copy_mT(b + 1, (s + 1) % 2)
                        for gg, i in jobs_at(g, s * NQ + j, 0):
                            evacuate(gg, i)
                        n = b * NQ + j
                        act.wait_ge(sc_filled, n + 1)
                        after(act, pv_filled, n - 1)
                        act.activation(pT[:, (s * NQ + j) % 2, :, :],
                                       sc_ps[(s * NQ + j) % 2][:, :].rearrange("p (h s) -> p h s", h=QH),
                                       ACT.Exp, scale=SCALE).then_inc(exp_done, 1)
                        for gg, i in jobs_at(g, s * NQ + j, 1):
                            evacuate(gg, i)
                        if j == OT_AT and (s or not (isinstance(g, int) and g == 0)):
                            copy_oT(b - 1)

            def copy_oT(b):
                act.wait_ge(oT_filled, b + 1)
                after(act, y_filled, b)
                act.activation(oT[0][:, :, :], tail_ps[:, 0:3 * S].rearrange("p (k s) -> p k s", k=3), ACT.Copy)\
                   .then_inc(oT_hi_made, 1)

            groups(act, body)
            copy_oT(B - 1)

        @block.vector
        def _(dve):
            def reduce_max(b, j):
                dve.wait_ge(max_filled, b * NQ + j + 1)
                sc = max_ps[j % 2][:, :].rearrange("p (h t) -> p h t", h=QH)
                hs = slice(j * QH, (j + 1) * QH)
                for s, (a, e) in enumerate(SEGS):
                    last = dve.tensor_reduce(m_seg[:, hs, s:s + 1], sc[:, :, a:e], axis=AX.X, op=ALU.max)
                last.then_inc(max_reduced, 1)

            def negate(b):
                dve.wait_ge(max_reduced, (b + 1) * NQ)
                after(dve, mT_filled, b)
                dve.tensor_scalar(nm[:, :, 0, :], m_seg[:, :, :], -1.0, None, ALU.mult).then_inc(nm_hi_made, 1)
                dve.wait_ge(nm_hi_made, b + 1)
                dve.scalar_tensor_tensor(out=nm[:, :, 1, :], in0=m_seg[:, :, :], scalar=-1.0, in1=nm[:, :, 0, :],
                                         op0=ALU.mult, op1=ALU.subtract).then_inc(nm_made, 1)

            def subtract_part(g, n):
                kind, m = SPLITS[n]
                r = split_rows(n)
                dve.wait_ge(part1_made, g * NSP + n + 1)
                after(dve, part3_made, g * NSP + n - 1)
                dve.tensor_tensor(rest[0:r, n % 2, :], job_ps[0:r, :], parts[0:r, n % 2, 0, :], ALU.subtract)\
                   .then_inc(job_freed, 1)

            def normalise(n, i, s, j):
                dve.wait_ge(pv_filled, n + 1)
                pv = pv_ps[i][:, 0:QH * NSEG * WS].rearrange("p (h a w) -> p h a w", h=QH, a=NSEG)
                after(dve, normalised, n)
                dve.reciprocal(rl[:, :, :, :], pv[:, :, :, D:W]).then_inc(rl_made, 1)
                dve.wait_ge(rl_made, n + 1)
                if j == 0:
                    after(dve, o_two_made, (n - NQ) // NQ if isinstance(n, int) else merged_before[0])
                dve.tensor_tensor(o_seg[:, s % 2, :, j * QH:(j + 1) * QH, :].rearrange("p a h d -> p h a d"),
                                  pv[:, :, :, 0:D], rl[:, :, :, :].broadcast_to((P, QH, NSEG, D)), ALU.mult)\
                   .then_inc(normalised, 1)

            merged_before = [0]

            def subtract_hi(g, n):
                kind, i = JOBS[n]
                nk = CK if kind == "ctx" else 3
                dve.wait_ge(hi_made, g * 2 * NB + (i if kind == "ctx" else NB + i) + 1)
                dve.tensor_tensor(aT[1][:, 0:nk, i, :], job_ps[:, 0:nk * S].rearrange("p (k t) -> p k t", k=nk),
                                  aT[0][:, 0:nk, i, :].bitcast(fp32), ALU.subtract).then_inc(job_freed, 1)

            def subtract_oT(b):
                dve.wait_ge(oT_hi_made, b + 1)
                dve.tensor_tensor(oT[1][:, :, :], tail_ps[:, 0:3 * S].rearrange("p (k s) -> p k s", k=3),
                                  oT[0][:, :, :].bitcast(fp32), ALU.subtract).then_inc(oT_copied, 1)

            def dve_job(g, n):
                if JOBS[n][0] in ("ctx", "x"):
                    subtract_hi(g, n)
                elif JOBS[n] in SPLITS:
                    subtract_part(g, SPLITS.index(JOBS[n]))

            def add_residual(g, s, b):
                dve.wait_ge(y_filled, b + 1)
                dve.wait_ge(x_res_made, b + 1)
                after(dve, y_stored[s % 2], (g * (NB // 2) + s // 2) * 16)
                dve.tensor_tensor(y[:, s % 2, :], tail_ps[:, 0:C], x_res[:, s, :], ALU.add).then_inc(y_made, 1)

            for n in range(HM // 2):
                if n == 0:
                    dve.wait_ge(consts_made, 10)
                dve.wait_ge(shift_loaded, 16 * (n + 1))
                dve.tensor_copy(shift_w[0:HM * RM, 2 * n:2 * n + 2, :], shift_f.rearrange("p (h t) -> p h t", h=2))\
                   .then_inc(consts_cast, 1)
            for n, (raw, w_parts) in enumerate(W_SPLITS):
                dve.wait_ge(w_hi_made, n + 1)
                dve.tensor_tensor(w_parts[1], raw, w_parts[0].bitcast(fp32), ALU.subtract).then_inc(w_lo_made, 1)
            for g, n in FIRST_JOBS:
                dve_job(g, n)
            for j in range(NQ):
                reduce_max(0, j)
            negate(0)

            def body(g):
                for s in range(NB):
                    b = g * NB + s
                    for j in range(NQ):
                        nxt = not (is_last(g) and s == NB - 1)
                        if nxt:
                            for jj in range(NQ):
                                if MAX_AT[jj] == j:
                                    reduce_max(b + 1, jj)
                            if MAX_AT[NQ - 1] == j:
                                negate(b + 1)
                        for half in range(2):
                            for gg, i in jobs_at(g, s * NQ + j, half):
                                dve_job(gg, i)
                        if s or j or not (isinstance(g, int) and g == 0):
                            q = s * NQ + j - 1
                            merged_before[0] = b - 1
                            ss, jj = divmod(q % (NB * NQ), NQ)
                            normalise(b * NQ + j - 1, q % 2, ss, jj)
                        if j == OT_AT and (s or not (isinstance(g, int) and g == 0)):
                            subtract_oT(b - 1)
                        if j == Y_AT and (s or not (isinstance(g, int) and g == 0)):
                            pg = g if s else g - 1
                            add_residual(pg, (s - 1) % NB, b - 1)

            groups(dve, body)
            normalise(B * NQ - 1, 1, NB - 1, NQ - 1)
            subtract_oT(B - 1)
            add_residual(G - 1, NB - 1, B - 1)

        @block.tensor
        def _(pe):
            PASSES = ((0, 0), (0, 1), (1, 0))

            def passes(dst, pairs):
                last = None
                for i, (w, m) in enumerate(pairs):
                    for a, c in PASSES:
                        last = pe.matmul(dst, w[a], m[c], start=(i == 0 and (a, c) == PASSES[0]),
                                         stop=(i == len(pairs) - 1 and (a, c) == PASSES[-1]))
                return last

            def small_job(i, n):
                after(pe, job_freed, i * (NB + MKV) + n)
                if n < NB:
                    if n == 0:
                        pe.wait_ge(c_loaded, (i + 1) * 16)
                    for k in range(CK):
                        last = pe.transpose(job_ps[:, k * P:(k + 1) * P], c_in[:, n, k * P:(k + 1) * P], ident[:, :])
                else:
                    m = n - NB
                    for k in range(CK):
                        last = pe.matmul(job_ps[:, :], w_small[:, i, k, m * P:(m + 1) * P],
                                         cT_small[:, k, :, :].rearrange("p t b -> p (t b)"),
                                         start=(k == 0), stop=(k == CK - 1))
                last.then_inc(job_filled, 1)

            def job(g, n):
                kind, i = JOBS[n]
                pe.wait_ge(job_freed, jobs_before(g, n))
                if kind == "ctx":
                    if i == 0:
                        pe.wait_ge(c_loaded, (len(SMALL) + g + 1) * 16)
                    for k in range(CK):
                        last = pe.transpose(job_ps[:, k * T:(k + 1) * T], c_in[:, i, k * P:(k + 1) * P], ident[:, :])
                elif kind == "x":
                    if i == 0:
                        pe.wait_ge(x_loaded, (g + 1) * 16)
                    for k, at in enumerate((0, P, C - P)):
                        last = pe.transpose(job_ps[:, k * S:(k + 1) * S], x_in[:, i, at:at + P], ident[:, :])
                elif kind == "kv":
                    ps = job_ps[:, :].rearrange("p (b t) -> p b t", b=NB)
                    for l, s in enumerate(LARGE):
                        a, e = WIDE[s]
                        passes(ps[:, :, a:e], [([w[:, l, k, i * P:(i + 1) * P] for w in w_kv],
                                                [t[:, k, :, a:e] for t in aT]) for k in range(CK)])
                    if i == 0:
                        pe.wait_ge(small_loaded, (g + 1) * 16)
                    last = pe.matmul(ps[:, :, SA:SE], ident[:, :], small[:, i, :, :], start=True, stop=True)
                elif kind == "q":
                    last = passes(job_ps[:, :], [([w[f:P, k, i * P:(i + 1) * P] for w in w_q],
                                                  [t[f:P, k, :, :].rearrange("p b s -> p (b s)") for t in aT])
                                                 for k, f in enumerate((0, 0, P - CT))])
                else:
                    for k in range(1, 3):
                        pe.transpose(job_ps[:, CT + (k - 1) * P:CT + k * P], vT[:, k, i, :], ident[:, :])
                    last = pe.transpose(job_ps[:, 0:CT], vT[CT:P, 0, i, :], ident[CT:P, CT:P])
                last.then_inc(job_filled, 1)

            def max_scores(g, s, b, j):
                if j == 0 and s % 2 == 0:
                    pe.wait_ge(stack_loaded[s // 2], (g + 1) * 16 * 2 * SLOTS)
                if j == 1:
                    after(pe, mT_copied, b)
                elif j == 0:
                    after(pe, max_reduced, b * NQ)
                else:
                    pe.wait_ge(max_reduced, b * NQ + j - 1)
                for h in range(QH):
                    hh = j * QH + h
                    last = pe.matmul(max_ps[j % 2][:, h * T:(h + 1) * T], q_st[s // 2][:, hh, s % 2, :],
                                     k_st[s // 2][:, hh, s % 2, :], start=True, stop=True)
                last.then_inc(max_filled, 1)

            def transpose_shifts(b):
                pe.wait_ge(nm_made, b + 1)
                v = nm[:, :, :, :].rearrange("p (a h) r s -> p a (h r s)", a=2)
                for a in range(2):
                    last = pe.transpose(mT_ps[0:HM * RM, a * S:(a + 1) * S], v[:, a, :], ident_b[:, :])
                last.then_inc(mT_filled, 1)

            def scores(s, b, j):
                i = (s * NQ + j) % 2
                if j == 0:
                    pe.wait_ge(mT_copied, b + 1)
                after(pe, exp_done, b * NQ + j - 1)
                for h in range(QH):
                    hh = j * QH + h
                    dst = sc_ps[i][:, h * S:(h + 1) * S]
                    pe.matmul(dst, k_st[s // 2][:, hh, s % 2, :], q_st[s // 2][:, hh, s % 2, :], start=True, stop=False)
                    last = pe.matmul(dst, shift_w[:, hh % HM, :], mT[:, s % 2, hh // HM, :], start=False, stop=True)
                last.then_inc(sc_filled, 1)

            def values(g, s, j, n):
                i = (s * NQ + j) % 2
                pe.wait_ge(exp_done, n + 1)
                if j == 0 and s % 2 == 0:
                    pe.wait_ge(v_seg_loaded[s // 2], (g + 1) * 16 * N_VD)
                after(pe, normalised, n - 1)
                for h in range(QH):
                    hh = j * QH + h
                    last = pe.matmul(pv_ps[i][:, h * NSEG * WS:(h + 1) * NSEG * WS], pT[:, i, h, :],
                                     v_seg[s // 2][:, s % 2, :, hh * W:hh * W + WS], start=True, stop=True)
                last.then_inc(pv_filled, 1)

            def transpose_o(b):
                pe.wait_ge(o_made, b + 1)
                after(pe, y_made, b)
                for k, at in enumerate((0, P, C - P)):
                    last = pe.transpose(tail_ps[:, k * S:(k + 1) * S], o[:, at:at + P], ident[:, :])
                last.then_inc(oT_filled, 1)

            def project(b):
                pe.wait_ge(oT_copied, b + 1)
                last = passes(tail_ps[:, 0:C], [([t[f:P, k, :] for t in oT], [w[f:P, k, :] for w in w_o])
                                                for k, f in enumerate((0, 0, P - CT))])
                last.then_inc(y_filled, 1)

            pe.wait_ge(w_loaded, 16 * N_W)
            pe.wait_ge(consts_made, 10)
            pe.wait_ge(consts_cast, HM // 2)
            for i in range(len(SMALL)):
                for n in range(NB + MKV):
                    small_job(i, n)
            pe.wait_ge(w_lo_made, len(W_SPLITS))
            for g, n in FIRST_JOBS:
                job(g, n)
            pe.wait_ge(pads_made, 2)
            for j in range(NQ):
                max_scores(0, 0, 0, j)
            transpose_shifts(0)

            def body(g):
                for s in range(NB):
                    b = g * NB + s
                    begun = s or not (isinstance(g, int) and g == 0)
                    for j in range(NQ):
                        if not (is_last(g) and s == NB - 1):
                            for jj in range(NQ):
                                if MAX_AT[jj] == j:
                                    max_scores(g if s < NB - 1 else g + 1, (s + 1) % NB, b + 1, jj)
                        if j == MT_AT and not (is_last(g) and s == NB - 1):
                            transpose_shifts(b + 1)
                        for gg, i in jobs_at(g, s * NQ + j, 0):
                            job(gg, i)
                        scores(s, b, j)
                        for gg, i in jobs_at(g, s * NQ + j, 1):
                            job(gg, i)
                        if j:
                            values(g, s, j - 1, b * NQ + j - 1)
                        elif begun:
                            values(g if s else g - 1, (s - 1) % NB, NQ - 1, b * NQ - 1)
                        if j == OT_AT and begun:
                            transpose_o(b - 1)
                        if j == Y_AT and begun:
                            project(b - 1)

            groups(pe, body)
            values(G - 1, NB - 1, NQ - 1, B * NQ - 1)
            transpose_o(B - 1)
            project(B - 1)


_X = "L0_xattn_"
_INS = ["x", "ctx_2048"] + [_X + n for n in (
    "to_q_w", "to_k_w", "to_v_w", "to_k_object_w", "to_v_object_w", "to_k_others_w", "to_v_others_w",
    "to_k_ip_w", "to_v_ip_w", "to_out_w", "to_out_b")]


def kernel(**inputs):
    import numpy as _np
    import concourse.bacc as _bacc
    from concourse import mybir as _mybir
    from concourse.bass_utils import run_bass_kernel_spmd as _run

    nc = _bacc.Bacc("TRN2", target_bir_lowering=False, num_devices=1)
    arrays, args = {}, []
    for name in _INS:
        a = _np.ascontiguousarray(inputs[name])
        arrays[f"in_{name}"] = a
        args.append(nc.dram_tensor(f"in_{name}", a.shape, _mybir.dt.from_np(a.dtype), kind="ExternalInput").ap())
    rows = _np.zeros((HM, 2, NSEG, HM, T), _np.float32)
    for h in range(HM):
        for s, (a, e) in enumerate(SEGS):
            rows[h, :, s, h, a:e] = 1.0
    arrays["in_shift_rows"] = rows.reshape(HM * RM, HM * T)
    args.append(nc.dram_tensor("in_shift_rows", (HM * RM, HM * T), _mybir.dt.float32, kind="ExternalInput").ap())
    args.append(nc.dram_tensor("out_0", (B, S, C), _mybir.dt.float32, kind="ExternalOutput").ap())
    xattn_kernel(nc, *args)
    r = _run(nc, [arrays], core_ids=[0])
    return r.results[0]["out_0"]
```

```python
import concourse.bass as bass
from concourse import mybir
from contextlib import ExitStack

B, S, T = 128, 128, 128
C, CA = 320, 512
H = 20
D = C // H
SEGS = [(0, 77), (77, 81), (81, 85), (85, 128)]
NSEG = len(SEGS)
SCALE = 1.0 / float(D) ** 0.5

P = 128
NB = 4
G = B // NB
QH = 4
NQ = H // QH
NPAIR = NB // 2
SLOTS = 6
Q_PART = [0, 0, 0, 1, 1, 2]
K_PART = [0, 1, 2, 0, 1, 0]
KS = SLOTS * D
HM = H // 2
WS = 24
RM = 2 * NSEG
W = D + 1
CK = CA // P
MKV = 2 * C // P
CT = C - 2 * P

SMALL = [1, 2]
LARGE = [0, 3]
SA, SE = SEGS[SMALL[0]][0], SEGS[SMALL[-1]][1]
NSM = SE - SA
WIDE = {0: (0, SA + SA % 2), 3: (SE - SE % 2, T)}

JOBS = ([("ctx", b) for b in range(NB)] + [("kv", m) for m in range(MKV)] + [("x", b) for b in range(NB)]
        + [("q", m) for m in range(3)] + [("v", b) for b in range(NB)])
JOB_AT = [50, 53, 56, 59] + [1, 4, 7, 10, 12] + [14, 17, 20, 23] + [26, 29, 32] + [35, 38, 41, 44]
EARLY = NB
NJ = len(JOBS)
SMALL_JOBS = len(SMALL) * (NB + MKV)
SPLITS = [("kv", 0), ("kv", 1), ("kv", 2), ("q", 0), ("q", 1), ("q", 2)]
NSP = len(SPLITS)
PR = 3
OT_AT, Y_AT = [2, 3, 3, 3], [3, 4, 4, 4]
MAX_AT = [[0, 1, 1, 2, 3], [-1, 0, 1, 2, 3], [0, 1, 1, 2, 3], [0, 1, 1, 2, 3]]
MT_AT = 4


def job_no(kind, i):
    return JOBS.index((kind, i))


def jobs_at(g, pos, turn):
    found = [(g + 2 if n < EARLY else g + 1, n) for n in range(NJ) if JOB_AT[n] == 3 * pos + turn]
    return [(gg, n) for gg, n in found if not isinstance(gg, int) or gg < G]


def jobs_before(g, n):
    return SMALL_JOBS + g * NJ + n


def max_at(g, s, j):
    found = ([(1, q) for q in range(NQ) if MAX_AT[s][q] == j]
             + [(2, q) for q in range(NQ) if MAX_AT[(s + 1) % NB][q] + NQ == j])
    return [(a, q) for a, q in found if not (isinstance(g, int) and g == G - 1 and s + a >= NB)]


def v_seg_pieces():
    pieces = []
    for s, (a, e) in enumerate(SEGS):
        while a < e:
            n = e - a if e - a < 16 else 16 * ((e - a) // 16)
            pieces.append((s, a, n))
            a += n
    return pieces


N_VD = len(v_seg_pieces())
VR = (H - 1) * W + WS + 1


def split_rows(n):
    return CT if SPLITS[n][1] == 2 else P


def xattn_kernel(nc: bass.Bass, x, ctx_in, wq, wk, wv, wko, wvo, wkt, wvt, wki, wvi, wo, bo, shift_rows, out):
    fp32 = mybir.dt.float32
    fp32r = mybir.dt.float32r
    bf16 = mybir.dt.bfloat16
    ALU = mybir.AluOpType
    ACT = mybir.ActivationFunctionType
    AX = mybir.AxisListType

    q_scr = nc.dram_tensor("q_scratch", [G, 3, C, NB * S], bf16, kind="Internal").ap()
    k_scr = nc.dram_tensor("k_scratch", [G, 3, C, NB * T], bf16, kind="Internal").ap()

    small_scr = nc.dram_tensor("small_scratch", [G, P, MKV * NB * NSM], fp32, kind="Internal").ap()

    with ExitStack() as stack:
        def sb(name, shape, dt=fp32):
            return stack.enter_context(nc.sbuf_tensor(name, shape, dt))

        def bank(name):
            return stack.enter_context(nc.psum_tensor(name, [P, 512], fp32))

        def sem(name):
            return stack.enter_context(nc.semaphore(name))

        x_in = sb("x_in", [P, NB, C + CT])
        x_park = sb("x_park", [P, C])
        x_res = sb("x_res", [P, NB, C])
        c_in = sb("c_in", [P, NB, CA])
        aT = [sb(f"aT{i}", [P, CK, NB, S], fp32r) for i in range(2)]
        vT = sb("vT", [P, 3, NB, T])
        w_kv = [sb(f"w_kv{i}", [P, len(LARGE), CK, 2 * C], fp32r) for i in range(2)]
        w_q = [sb(f"w_q{i}", [P, 3, 3 * P], fp32r) for i in range(2)]
        w_o = [sb(f"w_o{i}", [P, 3, C], fp32r) for i in range(2)]
        small = sb("small", [P, MKV, NB, NSM])
        bias = sb("bias", [P, C])
        ident = sb("ident", [P, P])
        zero = sb("zero", [P, 1])
        ident_b = sb("ident_b", [P, P], bf16)
        shift_w = sb("shift_w", [P, HM, T], bf16)
        parts = sb("parts", [P, PR, 3, NB * S], bf16)
        rest = sb("rest", [P, 2, NB * S])
        shift_f = rest[0:HM * RM, :, :].rearrange("p a n -> p (a n)")[:, 0:HM // 2 * T]
        q_all = sb("q_all", [P, NPAIR * H * 2 * S], bf16)
        k_all = sb("k_all", [P, NPAIR * H * 2 * T], bf16)
        q_st, k_st = ([t[:, i * H * 2 * S:(i + 1) * H * 2 * S].rearrange("p (h b n) -> p h b n", h=H, b=2)
                       for i in range(NPAIR)] for t in (q_all, k_all))
        m_seg = sb("m_seg", [P, H, NSEG])
        nm = sb("nm", [P, H, 2, NSEG], bf16)
        mT = sb("mT", [P, 2, 2, S], bf16)
        pT = sb("pT", [P, 2, QH, S])
        v_new = sb("v_new", [P, NPAIR, 2, H, W])
        v_all = sb("v_all", [P, NPAIR * 2 * NSEG * VR])
        v_seg = [v_all[:, i * 2 * NSEG * VR:(i + 1) * 2 * NSEG * VR]
                 .rearrange("p (b a w) -> p b a w", b=2, a=NSEG) for i in range(NPAIR)]
        rl = sb("rl", [P, QH, NSEG, 1])
        o_seg = sb("o_seg", [P, 2, NSEG, H, D])
        o = sb("o", [P, C + CT])
        oT = [sb(f"oT{i}", [P, 3, S], fp32r) for i in range(2)]
        y = sb("y", [P, 2, C])

        w_small = q_all[:, :].bitcast(fp32).rearrange("p (s k c) -> p s k c", s=len(SMALL), k=CK)
        w_large = k_all[:, :].bitcast(fp32).rearrange("p (s k c) -> p s k c", s=len(LARGE), k=CK)
        parts_flat = parts[:, :, :, :].rearrange("p r a n -> p (r a n)").bitcast(fp32)
        wq_raw = parts_flat[:, 0:3 * C].rearrange("p (k c) -> p k c", k=3)
        wo_raw = parts_flat[:, 3 * C:6 * C].rearrange("p (k c) -> p k c", k=3)
        small_all = v_all[:, 0:G * MKV * NB * NSM].rearrange("p (g m b t) -> p g m b t", g=G, m=MKV, b=NB)
        o_seg_flat = o_seg[:, :, :, :, :].rearrange("p b a h d -> p (b a h d)")
        cT_small = o_seg_flat[:, 0:CK * NB * P].rearrange("p (k t b) -> p k t b", k=CK, t=NB)

        max_ps = [bank(f"max_ps{i}") for i in range(2)]
        sc_ps = [bank(f"sc_ps{i}") for i in range(2)]
        pv_ps = [bank(f"pv_ps{i}") for i in range(2)]
        job_ps = bank("job_ps")
        tail_ps = bank("tail_ps")
        mT_ps = max_ps[1][:, :].bitcast(bf16)

        w_loaded = sem("w_loaded")
        w_small_loaded = sem("w_small_loaded")
        consts_made = sem("consts_made")
        shift_loaded = sem("shift_loaded")
        consts_cast = sem("consts_cast")
        x_loaded = sem("x_loaded")
        c_loaded = sem("c_loaded")
        w_hi_made = sem("w_hi_made")
        w_lo_made = sem("w_lo_made")
        hi_made = sem("hi_made")
        oT_hi_made = sem("oT_hi_made")
        small_stored = sem("small_stored")
        small_loaded = sem("small_loaded")
        pads_made = sem("pads_made")
        v_cleared = sem("v_cleared")
        job_filled = sem("job_filled")
        job_freed = sem("job_freed")
        part1_made = sem("part1_made")
        part2_made = sem("part2_made")
        part3_made = sem("part3_made")
        parts_stored = [sem(f"parts_stored{i}") for i in range(PR)]
        q_tail_loaded = sem("q_tail_loaded")
        stack_loaded = [sem(f"stack_loaded{i}") for i in range(NPAIR)]
        v_seg_loaded = [sem(f"v_seg_loaded{i}") for i in range(NPAIR)]
        max_filled = sem("max_filled")
        max_reduced = sem("max_reduced")
        nm_hi_made = sem("nm_hi_made")
        nm_made = sem("nm_made")
        mT_filled = sem("mT_filled")
        mT_copied = sem("mT_copied")
        sc_filled = sem("sc_filled")
        exp_done = sem("exp_done")
        pv_filled = sem("pv_filled")
        rl_made = sem("rl_made")
        normalised = sem("normalised")
        o_two_made = sem("o_two_made")
        o_made = sem("o_made")
        oT_filled = sem("oT_filled")
        oT_copied = sem("oT_copied")
        y_filled = sem("y_filled")
        y_made = sem("y_made")
        x_res_made = sem("x_res_made")
        x_parked = sem("x_parked")
        v_head_copied = sem("v_head_copied")
        y_stored = [sem(f"y_stored{i}") for i in range(2)]

        block = stack.enter_context(nc.Block())

        def after(eng, s, value):
            if not isinstance(value, int) or value > 0:
                eng.wait_ge(s, value)

        def groups(eng, body):
            body(0)
            with eng.Fori(1, G - 2) as g:
                body(g)
            body(G - 2)
            body(G - 1)

        def is_last(g):
            return isinstance(g, int) and g == G - 1

        HQ = 2 * P // D
        CASTS = 2
        HC = HM // CASTS
        FIRST_PS = [job_ps, tail_ps]
        FIRST_JOBS = [(0, n) for n in range(NJ)] + [(1, n) for n in range(EARLY)]
        seg_w = [(wk, wv), (wko, wvo), (wkt, wvt), (wki, wvi)]
        N_W = 2 * len(LARGE) + 2 * 3 + 1
        W_FIRST = [(w_large, w_kv[0][:, :, :, :]),
                   (wq_raw[:, 0:2, :], w_q[0][:, 0:2, 0:C]), (wq_raw[P - CT:P, 2, :], w_q[0][P - CT:P, 2, 0:C]),
                   (wq_raw[0:CT, 2, :], w_q[1][0:CT, 2, 0:C]),
                   (wo_raw[:, 0:2, :], w_o[0][:, 0:2, :]), (wo_raw[P - CT:P, 2, :], w_o[0][P - CT:P, 2, :]),
                   (wo_raw[0:CT, 2, :], w_o[1][0:CT, 2, :])]
        W_SECOND = [(w_large, w_kv[0][:, :, :, :], w_kv[1][:, :, :, :]),
                    (wq_raw[:, 0:2, :], w_q[0][:, 0:2, 0:C], w_q[1][:, 0:2, 0:C]),
                    (wq_raw[0:CT, 2, :], w_q[1][0:CT, 2, 0:C], w_q[0][0:CT, 2, 0:C]),
                    (wo_raw[:, 0:2, :], w_o[0][:, 0:2, :], w_o[1][:, 0:2, :]),
                    (wo_raw[0:CT, 2, :], w_o[1][0:CT, 2, :], w_o[0][0:CT, 2, :])]

        @block.sync
        def _(sp):
            def load_c(g):
                sp.wait_ge(job_filled, SMALL_JOBS - MKV if isinstance(g, int) and g == 0 else jobs_before(g - 1, NB))
                sp.dma_start(c_in[:, :, :], ctx_in[bass.ts(g, NB)].rearrange("b t c -> t b c")).then_inc(c_loaded, 16)

            def load_small(g):
                if not (isinstance(g, int) and g == 0):
                    sp.wait_ge(job_filled, jobs_before(g - 1, NB + MKV))
                sp.dma_start(small[:, :, :, :].rearrange("p m b t -> p (m b t)"), small_scr[g]).then_inc(small_loaded, 16)

            def load_x(g):
                rows = x[bass.ts(g, NB)].rearrange("b s c -> s b c")
                sp.dma_start(x_in[:, :, 0:C], rows).then_inc(x_loaded, 16)
                sp.dma_start(x_in[:, :, C:C + CT], rows[:, :, 2 * P:C]).then_inc(x_loaded, 16)

            def store_parts(g, n):
                kind, m = SPLITS[n]
                r = split_rows(n)
                scr = q_scr if kind == "q" else k_scr
                sp.wait_ge(part3_made, g * NSP + n + 1)
                sp.dma_start(scr[g, :, m * P:m * P + r, :].rearrange("a c n -> c a n"),
                             parts[0:r, n % PR, :, :]).then_inc(parts_stored[n % PR], 16)

            def load_stack(g, h, st, scr, part, stored, h0, h1, loaded):
                for i in range(PR):
                    sp.wait_ge(parts_stored[i], (g * (NSP // PR) + (stored + PR - 1 - i) // PR) * 16)
                after(sp, sc_filled, (g * NB + 2 * h + 2 - NB) * NQ)
                for i in range(SLOTS):
                    sp.dma_start(st[h][i * D:(i + 1) * D, h0:h1, :, :].rearrange("d h b n -> d h (b n)"),
                                 scr[g, part[i], h0 * D:h1 * D, h * 2 * S:(h + 1) * 2 * S]
                                 .rearrange("(h d) n -> d h n", d=D)).then_inc(loaded, 16)

            def load_k(g, h):
                load_stack(g, h, k_st, k_scr, K_PART, 3, 0, H, stack_loaded[h])

            def load_q(g, h):
                load_stack(g, h, q_st, q_scr, Q_PART, NSP, 0, H, stack_loaded[h])

            def load_q_head(g):
                load_stack(g, 0, q_st, q_scr, Q_PART, NSP - 1, 0, HQ, stack_loaded[0])

            def load_q_tail(g):
                load_stack(g, 0, q_st, q_scr, Q_PART, NSP, HQ, H, q_tail_loaded)

            def load_v_seg(g, h):
                sp.wait_ge(v_cleared, 1)
                sp.wait_ge(job_freed, jobs_before(g, job_no("v", 2 * h + 1) + 1))
                after(sp, pv_filled, (g * NB + 2 * h + 2 - NB) * NQ)
                for s, a, n in v_seg_pieces():
                    sp.dma_start(v_seg[h][a:a + n, :, s, 0:H * W],
                                 v_new[a:a + n, h, :, :, :].rearrange("t b h w -> t b (h w)"))\
                      .then_inc(v_seg_loaded[h], 16)

            def store_y(b, parity):
                sp.wait_ge(y_made, b + 1)
                sp.dma_start(out[b], y[:, parity, :]).then_inc(y_stored[parity], 16)

            def load_small_c(i):
                a, e = SEGS[SMALL[i]]
                after(sp, job_filled, i * (NB + MKV) - MKV)
                sp.dma_start(c_in[:, :, :], ctx_in[:, a:e, :]).then_inc(c_loaded, 16)

            def load_w(w_raw, segs):
                for i, s in enumerate(segs):
                    loaded = w_small_loaded if segs is SMALL else w_loaded
                    for at, w in zip((0, C), seg_w[s]):
                        sp.dma_start(w_raw[:, i, :, at:at + C], w.rearrange("(k p) c -> p k c", p=P)).then_inc(loaded, 16)

            def load_shifts(n):
                after(sp, consts_cast, n)
                sp.dma_start(shift_f, shift_rows[:, n * HC * T:(n + 1) * HC * T]).then_inc(shift_loaded, 16)

            load_small_c(0)
            load_w(w_small, SMALL)
            load_w(w_large, LARGE)
            for w_sb, w in ((wq_raw, wq), (wo_raw, wo)):
                sp.dma_start(w_sb[:, 0:2, :], w[0:2 * P, :].rearrange("(k p) c -> p k c", p=P)).then_inc(w_loaded, 16)
                for at in (0, P - CT):
                    sp.dma_start(w_sb[at:at + CT, 2, :], w[2 * P:C, :]).then_inc(w_loaded, 16)
            sp.dma_start(bias[:, :], bo.rearrange("(a c) -> a c", a=1).broadcast_to((P, C))).then_inc(w_loaded, 16)
            load_x(0)
            load_shifts(0)
            load_small_c(1)
            load_c(0)
            load_shifts(1)
            sp.wait_ge(job_freed, SMALL_JOBS)
            def store_small(g0, g1):
                sp.dma_start(small_scr[g0:g1].rearrange("g p n -> p g n"),
                             small_all[:, g0:g1, :, :, :].rearrange("p g m b t -> p g (m b t)")).then_inc(small_stored, 16)

            store_small(0, 1)
            sp.wait_ge(small_stored, 16)
            load_small(0)
            store_small(1, G)
            for n in range(3):
                store_parts(0, n)
            load_c(1)
            load_k(0, 0)
            for n in range(3, NSP):
                store_parts(0, n)
            load_q_head(0)
            load_q_tail(0)
            sp.wait_ge(small_stored, 2 * 16)
            load_small(1)
            load_v_seg(0, 0)

            def body(g):
                begun = not (isinstance(g, int) and g == 0)
                more = not is_last(g)
                load_k(g, 1)
                load_q(g, 1)
                if more:
                    sp.wait_ge(x_res_made, (g + 1) * NB - 1)
                    sp.wait_ge(x_parked, g + 1)
                    load_x(g + 1)
                load_v_seg(g, 1)
                if not (isinstance(g, int) and g >= G - 2):
                    load_c(g + 2)
                if begun:
                    store_y(g * NB - 2, 0)
                if more:
                    for n in range(2):
                        store_parts(g + 1, n)
                if begun:
                    store_y(g * NB - 1, 1)
                if more:
                    store_parts(g + 1, 2)
                    if not (isinstance(g, int) and g == G - 2):
                        load_small(g + 2)
                    store_parts(g + 1, 3)
                store_y(g * NB, 0)
                if more:
                    store_parts(g + 1, 4)
                    load_k(g + 1, 0)
                    load_q_head(g + 1)
                    store_parts(g + 1, 5)
                    load_q_tail(g + 1)
                store_y(g * NB + 1, 1)
                if more:
                    load_v_seg(g + 1, 0)

            body(0)
            with sp.Fori(1, G - 2) as g:
                body(g)
            body(G - 2)
            body(G - 1)
            store_y(B - 2, 0)
            store_y(B - 1, 1)
            for i in range(2):
                sp.wait_ge(y_stored[i], 16 * B // 2)

        @block.gpsimd
        def _(pool):
            pool.memset(ident[:, :], 0.0).then_inc(consts_made, 1)
            pool.memset(ident_b[:, :], 0.0).then_inc(consts_made, 1)
            for t in w_q:
                pool.memset(t[:, :, C:3 * P].bitcast(fp32), 0.0).then_inc(consts_made, 1)
            pool.memset(v_new[:, :, :, :, :], 1.0).then_inc(consts_made, 1)
            pool.memset(zero[:, :], 0.0).then_inc(consts_made, 1)
            pool.memset(mT[:, :, :, :], 0.0).then_inc(consts_made, 1)
            pool.memset(shift_w[:, :, :], 0.0).then_inc(consts_made, 1)
            pool.wait_ge(consts_made, 8)
            for m in (ident, ident_b):
                pool.affine_select(out=m[:, :], in_=m[:, :], compare_op=ALU.not_equal, fill=1.0, base=0,
                                   pattern=[[-1, P]], channel_multiplier=1).then_inc(consts_made, 1)

            def split(g, n):
                r = split_rows(n)
                kind, m = SPLITS[n]
                src, dst = rest[0:r, n % 2, :], parts[0:r, n % PR, :, :]
                pool.wait_ge(job_freed, jobs_before(g, job_no(kind, m) + 1))
                after(pool, parts_stored[n % PR], (g * (NSP // PR) + n // PR) * 16)
                pool.tensor_tensor(dst[:, 1, :], src, zero[0:r, :].broadcast_to((r, NB * S)), ALU.add)\
                    .then_inc(part2_made, 1)
                pool.wait_ge(part2_made, g * NSP + n + 1)
                pool.tensor_tensor(dst[:, 2, :], src, dst[:, 1, :], ALU.subtract).then_inc(part3_made, 1)

            def add_bias(g, s):
                if s < NB - 1:
                    pool.wait_ge(x_loaded, (g + 1) * 16 * 2)
                else:
                    pool.wait_ge(x_parked, g + 1)
                after(pool, y_made, g * NB + s + 1 - NB)
                pool.tensor_tensor(x_res[:, s, :], x_in[:, s, 0:C] if s < NB - 1 else x_park[:, :], bias[:, :], ALU.add)\
                    .then_inc(x_res_made, 1)

            def park(g):
                pool.wait_ge(x_loaded, (g + 1) * 16 * 2)
                after(pool, x_res_made, g * NB)
                pool.tensor_tensor(x_park[:, :], x_in[:, NB - 1, 0:C], zero[:, :].broadcast_to((P, C)), ALU.add)\
                    .then_inc(x_parked, 1)

            def merge(b, parity):
                pool.wait_ge(normalised, (b + 1) * NQ)
                v = o_seg[:, parity, :, :, :].rearrange("p a h d -> p a (h d)")
                pool.tensor_tensor(v[:, 0:2, :], v[:, 0:2, :], v[:, 2:4, :], ALU.add).then_inc(o_two_made, 1)
                pool.wait_ge(o_two_made, b + 1)
                after(pool, oT_filled, b)
                pool.tensor_tensor(o[:, C:C + CT], v[:, 0, 2 * P:C], v[:, 1, 2 * P:C], ALU.add)
                pool.tensor_tensor(o[:, 0:C], v[:, 0, :], v[:, 1, :], ALU.add).then_inc(o_made, 1)

            for n, (raw, first, second) in enumerate(W_SECOND):
                pool.wait_ge(w_hi_made, 1 if n == 0 else len(W_FIRST))
                after(pool, w_lo_made, n)
                pool.tensor_tensor(second, raw, first.bitcast(fp32), ALU.subtract).then_inc(w_lo_made, 1)
            pool.wait_ge(w_lo_made, len(W_SECOND))
            for i, t in enumerate((k_all, q_all)):
                if i:
                    pool.wait_ge(job_filled, SMALL_JOBS)
                pool.memset(t[KS:P, :], 0.0).then_inc(pads_made, 1)
                pool.wait_ge(pads_made, i + 1)
            pool.wait_ge(w_loaded, 16 * N_W)
            for n in range(3):
                split(0, n)
            pool.wait_ge(small_stored, 2 * 16)
            pool.memset(v_all[:, :], 0.0).then_inc(v_cleared, 1)
            for n in range(3, NSP):
                split(0, n)
            for s in range(2):
                add_bias(0, s)

            def body(g):
                for s in range(NB):
                    b = g * NB + s
                    if s == 0:
                        add_bias(g, 2)
                        park(g)
                    if s == 1:
                        add_bias(g, 3)
                    if s or not (isinstance(g, int) and g == 0):
                        merge(b - 1, (s - 1) % 2)
                    if not is_last(g):
                        for n in range(NSP):
                            if JOB_AT[job_no(*SPLITS[n])] // (3 * NQ) == s:
                                split(g + 1, n)
                    if s >= 2 and not is_last(g):
                        add_bias(g + 1, s - 2)

            groups(pool, body)
            merge(B - 1, 1)

        @block.scalar
        def _(act):
            def evacuate(g, n, job_ps=job_ps):
                kind, i = JOBS[n]
                act.wait_ge(job_filled, jobs_before(g, n + 1))
                if kind == "v" or (kind == "kv" and i > 2):
                    act.wait_ge(job_freed, jobs_before(g, n))
                if kind == "ctx":
                    act.activation(aT[0][:, :, i, :], job_ps[:, :].rearrange("p (k t) -> p k t", k=CK), ACT.Copy)\
                       .then_inc(hi_made, 1)
                elif kind == "x":
                    act.activation(aT[0][:, 0:3, i, :], job_ps[:, 0:3 * S].rearrange("p (k t) -> p k t", k=3), ACT.Copy)\
                       .then_inc(hi_made, 1)
                elif kind == "v":
                    if i % 2 == 0:
                        after(act, v_seg_loaded[i // 2], g * 16 * N_VD)
                    if isinstance(g, int) and g == 0:
                        act.wait_ge(consts_made, 10)
                    act.activation(v_new[:, i // 2, i % 2, :, 0:D], job_ps[:, 0:C].rearrange("p (h d) -> p h d", d=D),
                                   ACT.Copy).then_inc(job_freed, 1)
                elif kind == "kv" and i > 2:
                    act.activation(vT[:, i - 2, :, :], job_ps[:, :].rearrange("p (b t) -> p b t", b=NB), ACT.Copy)\
                       .then_inc(job_freed, 1)
                else:
                    m = SPLITS.index((kind, i))
                    r = split_rows(m)
                    after(act, parts_stored[m % PR], (g * (NSP // PR) + m // PR) * 16)
                    act.activation(parts[0:r, m % PR, 0, :], job_ps[0:r, :], ACT.Copy).then_inc(part1_made, 1)
                    if (kind, i) == ("kv", 2):
                        act.activation(vT[CT:P, 0, :, :], job_ps[CT:P, :].rearrange("p (b t) -> p b t", b=NB), ACT.Copy)\
                           .then_inc(v_head_copied, 1)

            def copy_mT(b, parity):
                act.wait_ge(mT_filled, b + 1)
                after(act, sc_filled, (b - 1) * NQ)
                act.activation(mT[0:HM * RM, parity, :, :], mT_ps[0:HM * RM, 0:2 * S].rearrange("p (a s) -> p a s", a=2),
                               ACT.Copy).then_inc(mT_copied, 1)

            act.wait_ge(consts_made, 10)
            act.wait_ge(w_loaded, 16 * N_W)
            for raw, first in W_FIRST:
                act.activation(first, raw, ACT.Copy).then_inc(w_hi_made, 1)
            act.wait_ge(w_lo_made, len(W_SECOND))
            for i, (g, n) in enumerate(FIRST_JOBS):
                evacuate(g, n, FIRST_PS[i % 2])
            copy_mT(0, 0)

            def body(g):
                for s in range(NB):
                    b = g * NB + s
                    for j in range(NQ):
                        if j == MT_AT and not (is_last(g) and s == NB - 1):
                            copy_mT(b + 1, (s + 1) % 2)
                        for gg, i in jobs_at(g, s * NQ + j, 0):
                            evacuate(gg, i)
                        n = b * NQ + j
                        act.wait_ge(sc_filled, n + 1)
                        after(act, pv_filled, n - 1)
                        act.activation(pT[:, (s * NQ + j) % 2, :, :],
                                       sc_ps[(s * NQ + j) % 2][:, :].rearrange("p (h s) -> p h s", h=QH),
                                       ACT.Exp, scale=SCALE).then_inc(exp_done, 1)
                        for gg, i in jobs_at(g, s * NQ + j, 1):
                            evacuate(gg, i)
                        for gg, i in jobs_at(g, s * NQ + j, 2):
                            evacuate(gg, i)
                        if j == OT_AT[s] and (s or not (isinstance(g, int) and g == 0)):
                            copy_oT(b - 1)

            def copy_oT(b):
                act.wait_ge(oT_filled, b + 1)
                after(act, y_filled, b)
                act.activation(oT[0][:, :, :], tail_ps[:, 0:3 * S].rearrange("p (k s) -> p k s", k=3), ACT.Copy)\
                   .then_inc(oT_hi_made, 1)

            groups(act, body)
            copy_oT(B - 1)

        @block.vector
        def _(dve):
            def reduce_max(b, j):
                dve.wait_ge(max_filled, b * NQ + j + 1)
                sc = max_ps[j % 2][:, :].rearrange("p (h t) -> p h t", h=QH)
                hs = slice(j * QH, (j + 1) * QH)
                for s in LARGE:
                    a, e = SEGS[s]
                    dve.tensor_reduce(m_seg[:, hs, s:s + 1], sc[:, :, a:e], axis=AX.X, op=ALU.max)
                last = dve.tensor_reduce(m_seg[:, hs, SMALL[0]:SMALL[-1] + 1],
                                         sc[:, :, SA:SE].rearrange("p h (a t) -> p h a t", a=len(SMALL)),
                                         axis=AX.X, op=ALU.max)
                last.then_inc(max_reduced, 1)

            def negate(b):
                dve.wait_ge(max_reduced, (b + 1) * NQ)
                after(dve, mT_filled, b)
                dve.tensor_scalar(nm[:, :, 0, :], m_seg[:, :, :], -1.0, None, ALU.mult).then_inc(nm_hi_made, 1)
                dve.wait_ge(nm_hi_made, b + 1)
                dve.scalar_tensor_tensor(out=nm[:, :, 1, :], in0=m_seg[:, :, :], scalar=-1.0, in1=nm[:, :, 0, :],
                                         op0=ALU.mult, op1=ALU.subtract).then_inc(nm_made, 1)

            def subtract_part(g, n, job_ps=job_ps):
                kind, m = SPLITS[n]
                r = split_rows(n)
                dve.wait_ge(part1_made, g * NSP + n + 1)
                after(dve, part3_made, g * NSP + n - 1)
                dve.tensor_tensor(rest[0:r, n % 2, :], job_ps[0:r, :], parts[0:r, n % PR, 0, :], ALU.subtract)\
                   .then_inc(job_freed, 1)

            def normalise(n, i, s, j, merged):
                dve.wait_ge(pv_filled, n + 1)
                pv = pv_ps[i][:, 0:QH * NSEG * WS].rearrange("p (h a w) -> p h a w", h=QH, a=NSEG)
                after(dve, normalised, n)
                dve.reciprocal(rl[:, :, :, :], pv[:, :, :, D:W]).then_inc(rl_made, 1)
                dve.wait_ge(rl_made, n + 1)
                if j == 0:
                    after(dve, o_made, merged)
                dve.tensor_tensor(o_seg[:, s % 2, :, j * QH:(j + 1) * QH, :].rearrange("p a h d -> p h a d"),
                                  pv[:, :, :, 0:D], rl[:, :, :, :].broadcast_to((P, QH, NSEG, D)), ALU.mult)\
                   .then_inc(normalised, 1)

            def subtract_hi(g, n, job_ps=job_ps):
                kind, i = JOBS[n]
                nk = CK if kind == "ctx" else 3
                dve.wait_ge(hi_made, g * 2 * NB + (i if kind == "ctx" else NB + i) + 1)
                dve.tensor_tensor(aT[1][:, 0:nk, i, :], job_ps[:, 0:nk * S].rearrange("p (k t) -> p k t", k=nk),
                                  aT[0][:, 0:nk, i, :].bitcast(fp32), ALU.subtract).then_inc(job_freed, 1)

            def subtract_oT(b):
                dve.wait_ge(oT_hi_made, b + 1)
                dve.tensor_tensor(oT[1][:, :, :], tail_ps[:, 0:3 * S].rearrange("p (k s) -> p k s", k=3),
                                  oT[0][:, :, :].bitcast(fp32), ALU.subtract).then_inc(oT_copied, 1)

            def dve_job(g, n, job_ps=job_ps):
                if JOBS[n][0] in ("ctx", "x"):
                    subtract_hi(g, n, job_ps)
                elif JOBS[n] in SPLITS:
                    subtract_part(g, SPLITS.index(JOBS[n]), job_ps)

            def add_residual(g, s, b):
                dve.wait_ge(y_filled, b + 1)
                dve.wait_ge(x_res_made, b + 1)
                after(dve, y_stored[s % 2], (g * (NB // 2) + s // 2) * 16)
                dve.tensor_tensor(y[:, s % 2, :], tail_ps[:, 0:C], x_res[:, s, :], ALU.add).then_inc(y_made, 1)

            def cast_shifts(n):
                dve.wait_ge(shift_loaded, 16 * (n + 1))
                dve.tensor_copy(shift_w[0:HM * RM, HC * n:HC * (n + 1), :], shift_f.rearrange("p (h t) -> p h t", h=HC))\
                   .then_inc(consts_cast, 1)

            dve.wait_ge(consts_made, 10)
            for i in range(len(SMALL)):
                for n in range(NB + MKV):
                    m = i * (NB + MKV) + n
                    ps = FIRST_PS[m % 2]
                    dve.wait_ge(job_filled, m + 1)
                    if n < NB:
                        dve.tensor_copy(cT_small[:, :, n, :], ps[:, :].rearrange("p (k b) -> p k b", k=CK))\
                           .then_inc(job_freed, 1)
                    else:
                        k = SEGS[SMALL[i]][0] - SA
                        dve.tensor_copy(small_all[:, :, n - NB, :, k:k + NB].rearrange("p g b t -> p t g b"),
                                        ps[:, :].rearrange("p (t g b) -> p t g b", t=NB, g=G)).then_inc(job_freed, 1)
                    if n == NB:
                        cast_shifts(i)
            for i, (g, n) in enumerate(FIRST_JOBS):
                dve_job(g, n, FIRST_PS[i % 2])
            for j in range(NQ):
                reduce_max(0, j)
            negate(0)
            for j in range(NQ):
                if MAX_AT[0][j] < 0:
                    reduce_max(1, j)

            def body(g):
                for s in range(NB):
                    b = g * NB + s
                    for j in range(NQ):
                        for ahead, q in max_at(g, s, j):
                            reduce_max(b + ahead, q)
                            if q == NQ - 1:
                                negate(b + ahead)
                        for turn in range(2):
                            for gg, i in jobs_at(g, s * NQ + j, turn):
                                dve_job(gg, i)
                        if s or j or not (isinstance(g, int) and g == 0):
                            q = s * NQ + j - 1
                            ss, jj = divmod(q % (NB * NQ), NQ)
                            normalise(b * NQ + j - 1, q % 2, ss, jj, b - 1)
                        for gg, i in jobs_at(g, s * NQ + j, 2):
                            dve_job(gg, i)
                        if j == OT_AT[s] and (s or not (isinstance(g, int) and g == 0)):
                            subtract_oT(b - 1)
                        if j == Y_AT[s] and (s or not (isinstance(g, int) and g == 0)):
                            pg = g if s else g - 1
                            add_residual(pg, (s - 1) % NB, b - 1)

            groups(dve, body)
            normalise(B * NQ - 1, 1, NB - 1, NQ - 1, B - 2)
            subtract_oT(B - 1)
            add_residual(G - 1, NB - 1, B - 1)

        @block.tensor
        def _(pe):
            PASSES = ((0, 0), (0, 1), (1, 0))

            def passes(dst, pairs, stop=True):
                last = None
                for i, (w, m) in enumerate(pairs):
                    for a, c in PASSES:
                        last = pe.matmul(dst, w[a], m[c], start=(i == 0 and (a, c) == PASSES[0]),
                                         stop=(stop and i == len(pairs) - 1 and (a, c) == PASSES[-1]))
                return last

            def narrow(dst, pairs, tail):
                passes(dst, pairs, stop=False)
                (w, m), both = tail
                if both == "weights":
                    ops = [(w[0], m[0]), (w[0][P - CT:P], m[1][P - CT:P])]
                else:
                    ops = [(w[0], m[0]), (w[1][P - CT:P], m[0][P - CT:P])]
                for i, (a, c) in enumerate(ops):
                    last = pe.matmul(dst, a, c, start=False, stop=(i == 1))
                return last

            def small_job(i, n):
                m = i * (NB + MKV) + n
                job_ps = FIRST_PS[m % 2]
                after(pe, job_freed, m if n == NB else m - 1)
                if n < NB:
                    if n == 0:
                        pe.wait_ge(c_loaded, (i + 1) * 16)
                    for k in range(CK):
                        last = pe.transpose(job_ps[:, k * P:(k + 1) * P], c_in[:, n, k * P:(k + 1) * P], ident[:, :])
                else:
                    m = n - NB
                    if i == 0 and m == 0:
                        pe.wait_ge(w_small_loaded, 16 * 2 * len(SMALL))
                    for k in range(CK):
                        last = pe.matmul(job_ps[:, :], w_small[:, i, k, m * P:(m + 1) * P],
                                         cT_small[:, k, :, :].rearrange("p t b -> p (t b)"),
                                         start=(k == 0), stop=(k == CK - 1))
                last.then_inc(job_filled, 1)

            def job(g, n, job_ps=job_ps, others=0):
                kind, i = JOBS[n]
                pe.wait_ge(job_freed, jobs_before(g, n) - (0 if (kind, i) in (("kv", 0), ("q", 0)) else others))
                if kind == "kv" and i > 2:
                    pe.wait_ge(v_head_copied, g + 1)
                if kind == "ctx":
                    if i == 0:
                        pe.wait_ge(c_loaded, (len(SMALL) + g + 1) * 16)
                    for k in range(CK):
                        last = pe.transpose(job_ps[:, k * T:(k + 1) * T], c_in[:, i, k * P:(k + 1) * P], ident[:, :])
                elif kind == "x":
                    if i == 0:
                        pe.wait_ge(x_loaded, (g + 1) * 16 * 2)
                    for k in range(3):
                        last = pe.transpose(job_ps[:, k * S:(k + 1) * S], x_in[:, i, k * P:(k + 1) * P], ident[:, :])
                elif kind == "kv":
                    ps = job_ps[:, :].rearrange("p (b t) -> p b t", b=NB)
                    for l, s in enumerate(LARGE):
                        a, e = WIDE[s]
                        passes(ps[:, :, a:e], [([w[:, l, k, i * P:(i + 1) * P] for w in w_kv],
                                                [t[:, k, :, a:e] for t in aT]) for k in range(CK)])
                    if i == 0:
                        pe.wait_ge(small_loaded, (g + 1) * 16)
                    last = pe.matmul(ps[:, :, SA:SE], ident[:, :], small[:, i, :, :], start=True, stop=True)
                elif kind == "q":
                    ops = [([w[:, k, i * P:(i + 1) * P] for w in w_q],
                            [t[:, k, :, :].rearrange("p b s -> p (b s)") for t in aT]) for k in range(3)]
                    last = narrow(job_ps[:, :], ops[0:2], (ops[2], "weights"))
                else:
                    for k in range(1, 3):
                        pe.transpose(job_ps[:, CT + (k - 1) * P:CT + k * P], vT[:, k, i, :], ident[:, :])
                    last = pe.transpose(job_ps[:, 0:CT], vT[CT:P, 0, i, :], ident[CT:P, CT:P])
                last.then_inc(job_filled, 1)

            def max_scores(g, s, b, j):
                if j == 0 and s % 2 == 0:
                    pe.wait_ge(stack_loaded[s // 2], (g + 1) * 16 * 2 * SLOTS)
                if j == HQ // QH and s == 0:
                    pe.wait_ge(q_tail_loaded, (g + 1) * 16 * SLOTS)
                if j == 1:
                    after(pe, mT_copied, b)
                elif j == 0:
                    after(pe, max_reduced, b * NQ)
                else:
                    pe.wait_ge(max_reduced, b * NQ + j - 1)
                for h in range(QH):
                    hh = j * QH + h
                    last = pe.matmul(max_ps[j % 2][:, h * T:(h + 1) * T], q_st[s // 2][:, hh, s % 2, :],
                                     k_st[s // 2][:, hh, s % 2, :], start=True, stop=True)
                last.then_inc(max_filled, 1)

            def transpose_shifts(b):
                pe.wait_ge(nm_made, b + 1)
                v = nm[:, :, :, :].rearrange("p (a h) r s -> p a (h r s)", a=2)
                for a in range(2):
                    last = pe.transpose(mT_ps[0:HM * RM, a * S:(a + 1) * S], v[:, a, :], ident_b[:, :])
                last.then_inc(mT_filled, 1)

            def scores(s, b, j):
                i = (s * NQ + j) % 2
                if j == 0:
                    pe.wait_ge(mT_copied, b + 1)
                after(pe, exp_done, b * NQ + j - 1)
                for h in range(QH):
                    hh = j * QH + h
                    dst = sc_ps[i][:, h * S:(h + 1) * S]
                    pe.matmul(dst, k_st[s // 2][:, hh, s % 2, :], q_st[s // 2][:, hh, s % 2, :], start=True, stop=False)
                    last = pe.matmul(dst, shift_w[:, hh % HM, :], mT[:, s % 2, hh // HM, :], start=False, stop=True)
                last.then_inc(sc_filled, 1)

            def values(g, s, j, n):
                i = (s * NQ + j) % 2
                pe.wait_ge(exp_done, n + 1)
                if j == 0 and s % 2 == 0:
                    pe.wait_ge(v_seg_loaded[s // 2], (g + 1) * 16 * N_VD)
                after(pe, normalised, n - 1)
                for h in range(QH):
                    hh = j * QH + h
                    last = pe.matmul(pv_ps[i][:, h * NSEG * WS:(h + 1) * NSEG * WS], pT[:, i, h, :],
                                     v_seg[s // 2][:, s % 2, :, hh * W:hh * W + WS], start=True, stop=True)
                last.then_inc(pv_filled, 1)

            def transpose_o(b):
                pe.wait_ge(o_made, b + 1)
                after(pe, y_made, b)
                for k in range(3):
                    last = pe.transpose(tail_ps[:, k * S:(k + 1) * S], o[:, k * P:(k + 1) * P], ident[:, :])
                last.then_inc(oT_filled, 1)

            def project(b):
                pe.wait_ge(oT_copied, b + 1)
                ops = [([t[:, k, :] for t in oT], [w[:, k, :] for w in w_o]) for k in range(3)]
                last = narrow(tail_ps[:, 0:C], ops[0:2], (ops[2], "moving"))
                last.then_inc(y_filled, 1)

            pe.wait_ge(consts_made, 10)
            for i in range(len(SMALL)):
                for n in range(NB + MKV):
                    small_job(i, n)
            pe.wait_ge(w_lo_made, len(W_SECOND))
            for i, (g, n) in enumerate(FIRST_JOBS):
                job(g, n, FIRST_PS[i % 2], 1)
            pe.wait_ge(pads_made, 2)
            pe.wait_ge(consts_cast, CASTS)
            for j in range(NQ):
                max_scores(0, 0, 0, j)
            transpose_shifts(0)
            for j in range(NQ):
                if MAX_AT[0][j] < 0:
                    max_scores(0, 1, 1, j)

            def body(g):
                for s in range(NB):
                    b = g * NB + s
                    begun = s or not (isinstance(g, int) and g == 0)
                    for j in range(NQ):
                        for ahead, q in max_at(g, s, j):
                            max_scores(g + (s + ahead) // NB, (s + ahead) % NB, b + ahead, q)
                        if j == MT_AT and not (is_last(g) and s == NB - 1):
                            transpose_shifts(b + 1)
                        for gg, i in jobs_at(g, s * NQ + j, 0):
                            job(gg, i)
                        scores(s, b, j)
                        for gg, i in jobs_at(g, s * NQ + j, 1):
                            job(gg, i)
                        if j:
                            values(g, s, j - 1, b * NQ + j - 1)
                        elif begun:
                            values(g if s else g - 1, (s - 1) % NB, NQ - 1, b * NQ - 1)
                        for gg, i in jobs_at(g, s * NQ + j, 2):
                            job(gg, i)
                        if j == OT_AT[s] and begun:
                            transpose_o(b - 1)
                        if j == Y_AT[s] and begun:
                            project(b - 1)

            groups(pe, body)
            values(G - 1, NB - 1, NQ - 1, B * NQ - 1)
            transpose_o(B - 1)
            project(B - 1)


_X = "L0_xattn_"
_INS = ["x", "ctx_2048"] + [_X + n for n in (
    "to_q_w", "to_k_w", "to_v_w", "to_k_object_w", "to_v_object_w", "to_k_others_w", "to_v_others_w",
    "to_k_ip_w", "to_v_ip_w", "to_out_w", "to_out_b")]


def kernel(**inputs):
    import numpy as _np
    import concourse.bacc as _bacc
    from concourse import mybir as _mybir
    from concourse.bass_utils import run_bass_kernel_spmd as _run

    nc = _bacc.Bacc("TRN2", target_bir_lowering=False, num_devices=1)
    arrays, args = {}, []
    for name in _INS:
        a = _np.ascontiguousarray(inputs[name])
        arrays[f"in_{name}"] = a
        args.append(nc.dram_tensor(f"in_{name}", a.shape, _mybir.dt.from_np(a.dtype), kind="ExternalInput").ap())
    rows = _np.zeros((HM, 2, NSEG, HM, T), _np.float32)
    for h in range(HM):
        for s, (a, e) in enumerate(SEGS):
            rows[h, :, s, h, a:e] = 1.0
    arrays["in_shift_rows"] = rows.reshape(HM * RM, HM * T)
    args.append(nc.dram_tensor("in_shift_rows", (HM * RM, HM * T), _mybir.dt.float32, kind="ExternalInput").ap())
    args.append(nc.dram_tensor("out_0", (B, S, C), _mybir.dt.float32, kind="ExternalOutput").ap())
    xattn_kernel(nc, *args)
    r = _run(nc, [arrays], core_ids=[0])
    return r.results[0]["out_0"]
```
